# Optimizing a Trainium2 kernel written in Bass

```python
import numpy as np
import jax
import jax.numpy as jnp

def _softmax(x, axis=-1):
    return jax.nn.softmax(x, axis=axis)

def _gelu(x):
    return jax.nn.gelu(x, approximate=True)

def _silu(x):
    return jax.nn.silu(x)

def _sigmoid(x):
    return jax.nn.sigmoid(x)

def _layernorm(x, axis=-1, eps=1e-05):
    m = jnp.mean(x, axis=axis, keepdims=True)
    v = jnp.var(x, axis=axis, keepdims=True)
    return (x - m) / jnp.sqrt(v + eps)

def _scatter_add(tgt, idx, src, axis=0):
    return tgt.at[idx].add(src)

def _segment_sum(src, seg, n):
    return jax.ops.segment_sum(src, seg, n)
kernel_name = 'mk_gnn_preln_d2_gnn_r8_d5b516'

def setup_inputs(seed: int=0):
    np.random.seed(seed)
    _w = jnp.asarray

    def _rec_inputs():
        import jax
        import jax.numpy as jnp
        _gk = jax.random.key(seed)
        x = -0.0001126 + 1 * jax.random.normal(jax.random.fold_in(_gk, 1), (1250, 768), jnp.float32)
        _s = jax.random.randint(jax.random.fold_in(_gk, 2), (10000,), 0, 1250, jnp.int32)
        _d = jax.random.randint(jax.random.fold_in(_gk, 3), (10000,), 0, 1250, jnp.int32)
        _loop = jnp.arange(1250, dtype=jnp.int32)
        src = jnp.concatenate([_s, _d, _loop])
        dst = jnp.concatenate([_d, _s, _loop])
        _o = jnp.argsort(dst, stable=True)
        src = src[_o]
        dst = dst[_o]
        edge_type_3 = jax.random.randint(jax.random.fold_in(_gk, 12), (21250,), 0, 3, jnp.int32)
        node_type_3 = jax.random.randint(jax.random.fold_in(_gk, 13), (1250,), 0, 3, jnp.int32)
        return (x, src, dst, edge_type_3, node_type_3)
    x, src, dst, edge_type_3, node_type_3 = _rec_inputs()

    def _L0_gnn_setup():
        import jax, jax.numpy as jnp
        import numpy as np
        N = 1250
        E = 20000
        D = 768
        H1, C1 = (4, 192)
        H2, C2 = (2, 96)
        EPS = 1e-05
        NEG_SLOPE = 0.2

        def layer_norm(x, g, b):
            mu = x.mean(-1, keepdims=True)
            var = ((x - mu) ** 2).mean(-1, keepdims=True)
            return (x - mu) * jax.lax.rsqrt(var + EPS) * g + b

        def gat_conv(x, src, dst, W, a_src, a_dst, bias, H, C, n):
            h = (x @ W).reshape(n, H, C)
            s_src = (h * a_src).sum(-1)
            s_dst = (h * a_dst).sum(-1)
            e = jax.nn.leaky_relu(s_src[src] + s_dst[dst], NEG_SLOPE)
            emax = jax.ops.segment_max(e, dst, num_segments=n)
            ee = jnp.exp(e - emax[dst])
            denom = jax.ops.segment_sum(ee, dst, num_segments=n)
            alpha = ee / denom[dst]
            out = jax.ops.segment_sum(alpha[:, :, None] * h[src], dst, num_segments=n)
            return out.reshape(n, H * C) + bias
        key = jax.random.key(seed)
        ks = jax.random.split(key, 16)
        sd = 1.0 / np.sqrt(D)
        inp = {'x': jax.random.normal(ks[0], (N, D), jnp.float32), 'edge_index': jax.random.randint(ks[1], (2, E), 0, N, jnp.int64), 'norm_g': jnp.ones((D,), jnp.float32), 'norm_b': jnp.zeros((D,), jnp.float32), 'W1': jax.random.normal(ks[2], (D, H1 * C1), jnp.float32) * sd, 'a_src1': jax.random.normal(ks[3], (H1, C1), jnp.float32) * sd, 'a_dst1': jax.random.normal(ks[4], (H1, C1), jnp.float32) * sd, 'b1': jnp.zeros((H1 * C1,), jnp.float32), 'W2': jax.random.normal(ks[5], (H1 * C1, H2 * C2), jnp.float32) * sd, 'a_src2': jax.random.normal(ks[6], (H2, C2), jnp.float32) * sd, 'a_dst2': jax.random.normal(ks[7], (H2, C2), jnp.float32) * sd, 'b2': jnp.zeros((H2 * C2,), jnp.float32), 'Wu': jax.random.normal(ks[8], (D + H2 * C2, D), jnp.float32) / np.sqrt(D + H2 * C2), 'bu': jnp.zeros((D,), jnp.float32)}
        return inp
    _L0_gnn_all = _L0_gnn_setup()
    _L0_gnn_in = {k: v for k, v in _L0_gnn_all.items() if k in ('norm_g', 'norm_b', 'W1', 'a_src1', 'a_dst1', 'b1', 'W2', 'a_src2', 'a_dst2', 'b2', 'Wu', 'bu')}
    del _L0_gnn_all

    def _L1_gnn_setup():
        import jax, jax.numpy as jnp
        import numpy as np
        NUM_NODES = 1250
        NUM_EDGES = 20000
        IN_CH = 768
        TYPE_DIM = 128
        HID = 768
        OUT = 768
        NUM_REL = 3
        NUM_NODE_TYPE = 3

        def _glorot(key, shape):
            fan_in, fan_out = (shape[-2], shape[-1])
            lim = (6.0 / (fan_in + fan_out)) ** 0.5
            return jax.random.uniform(key, shape, jnp.float32, -lim, lim)

        def rgcn_conv(h, src, dst, edge_type, w_rel, w_root, bias):
            num_nodes = h.shape[0]
            xw = jnp.einsum('nd,rde->rne', h, w_rel)
            msg = xw[edge_type, src]
            onehot = jax.nn.one_hot(edge_type, NUM_REL, dtype=h.dtype)
            count = jax.ops.segment_sum(onehot, dst, num_segments=num_nodes)
            inv = jnp.where(count > 0, 1.0 / jnp.maximum(count, 1.0), 0.0)
            msg = msg * inv[dst, edge_type][:, None]
            agg = jax.ops.segment_sum(msg, dst, num_segments=num_nodes)
            return agg + h @ w_root + bias
        key = jax.random.key(seed)
        ks = jax.random.split(key, 16)
        d1 = IN_CH + TYPE_DIM
        inp = {'x': jax.random.normal(ks[0], (NUM_NODES, IN_CH), jnp.float32), 'node_type': jax.random.randint(ks[1], (NUM_NODES,), 0, NUM_NODE_TYPE, jnp.int32), 'edge_index': jax.random.randint(ks[2], (2, NUM_EDGES), 0, NUM_NODES, jnp.int32), 'edge_type': jax.random.randint(ks[3], (NUM_EDGES,), 0, NUM_REL, jnp.int32), 'node_emb': jax.random.normal(ks[4], (NUM_NODE_TYPE, TYPE_DIM), jnp.float32), 'w_rel1': _glorot(ks[5], (NUM_REL, d1, d1)), 'w_root1': _glorot(ks[6], (d1, d1)), 'b1': jnp.zeros((d1,), jnp.float32), 'w_rel2': _glorot(ks[7], (NUM_REL, d1, HID)), 'w_root2': _glorot(ks[8], (d1, HID)), 'b2': jnp.zeros((HID,), jnp.float32), 'w_rel3': _glorot(ks[9], (NUM_REL, HID, OUT)), 'w_root3': _glorot(ks[10], (HID, OUT)), 'b3': jnp.zeros((OUT,), jnp.float32)}
        return inp
    _L1_gnn_all = _L1_gnn_setup()
    _L1_gnn_in = {k: v for k, v in _L1_gnn_all.items() if k in ('node_emb', 'w_rel1', 'w_root1', 'b1', 'w_rel2', 'w_root2', 'b2', 'w_rel3', 'w_root3', 'b3')}
    del _L1_gnn_all
    return {'x': x, 'src': src, 'dst': dst, 'edge_type_3': edge_type_3, 'node_type_3': node_type_3, 'L0_gnn_norm_g': _L0_gnn_in['norm_g'], 'L0_gnn_norm_b': _L0_gnn_in['norm_b'], 'L0_gnn_W1': _L0_gnn_in['W1'], 'L0_gnn_a_src1': _L0_gnn_in['a_src1'], 'L0_gnn_a_dst1': _L0_gnn_in['a_dst1'], 'L0_gnn_b1': _L0_gnn_in['b1'], 'L0_gnn_W2': _L0_gnn_in['W2'], 'L0_gnn_a_src2': _L0_gnn_in['a_src2'], 'L0_gnn_a_dst2': _L0_gnn_in['a_dst2'], 'L0_gnn_b2': _L0_gnn_in['b2'], 'L0_gnn_Wu': _L0_gnn_in['Wu'], 'L0_gnn_bu': _L0_gnn_in['bu'], 'L1_gnn_node_emb': _L1_gnn_in['node_emb'], 'L1_gnn_w_rel1': _L1_gnn_in['w_rel1'], 'L1_gnn_w_root1': _L1_gnn_in['w_root1'], 'L1_gnn_b1': _L1_gnn_in['b1'], 'L1_gnn_w_rel2': _L1_gnn_in['w_rel2'], 'L1_gnn_w_root2': _L1_gnn_in['w_root2'], 'L1_gnn_b2': _L1_gnn_in['b2'], 'L1_gnn_w_rel3': _L1_gnn_in['w_rel3'], 'L1_gnn_w_root3': _L1_gnn_in['w_root3'], 'L1_gnn_b3': _L1_gnn_in['b3']}

def reference(x, src, dst, edge_type_3, node_type_3, L0_gnn_norm_g, L0_gnn_norm_b, L0_gnn_W1, L0_gnn_a_src1, L0_gnn_a_dst1, L0_gnn_b1, L0_gnn_W2, L0_gnn_a_src2, L0_gnn_a_dst2, L0_gnn_b2, L0_gnn_Wu, L0_gnn_bu, L1_gnn_node_emb, L1_gnn_w_rel1, L1_gnn_w_root1, L1_gnn_b1, L1_gnn_w_rel2, L1_gnn_w_root2, L1_gnn_b2, L1_gnn_w_rel3, L1_gnn_w_root3, L1_gnn_b3):
    import jax
    import jax.numpy as jnp

    def _L0_gnn_ref(x, edge_index, norm_g, norm_b, W1, a_src1, a_dst1, b1, W2, a_src2, a_dst2, b2, Wu, bu):
        import jax, jax.numpy as jnp
        import numpy as np
        N = 1250
        E = 20000
        D = 768
        H1, C1 = (4, 192)
        H2, C2 = (2, 96)
        EPS = 1e-05
        NEG_SLOPE = 0.2

        def layer_norm(x, g, b):
            mu = x.mean(-1, keepdims=True)
            var = ((x - mu) ** 2).mean(-1, keepdims=True)
            return (x - mu) * jax.lax.rsqrt(var + EPS) * g + b

        def gat_conv(x, src, dst, W, a_src, a_dst, bias, H, C, n):
            h = (x @ W).reshape(n, H, C)
            s_src = (h * a_src).sum(-1)
            s_dst = (h * a_dst).sum(-1)
            e = jax.nn.leaky_relu(s_src[src] + s_dst[dst], NEG_SLOPE)
            emax = jax.ops.segment_max(e, dst, num_segments=n)
            ee = jnp.exp(e - emax[dst])
            denom = jax.ops.segment_sum(ee, dst, num_segments=n)
            alpha = ee / denom[dst]
            out = jax.ops.segment_sum(alpha[:, :, None] * h[src], dst, num_segments=n)
            return out.reshape(n, H * C) + bias
        loops = jnp.arange(N, dtype=edge_index.dtype)
        src = jnp.concatenate([edge_index[0], loops])
        dst = jnp.concatenate([edge_index[1], loops])
        x_norm = layer_norm(x, norm_g, norm_b)
        out1 = gat_conv(x_norm, src, dst, W1, a_src1, a_dst1, b1, H1, C1, N)
        out2 = gat_conv(out1, src, dst, W2, a_src2, a_dst2, b2, H2, C2, N)
        combined = jnp.concatenate([x, out2], axis=-1)
        return combined @ Wu + bu

    def _L1_gnn_ref(x, node_type, edge_index, edge_type, node_emb, w_rel1, w_root1, b1, w_rel2, w_root2, b2, w_rel3, w_root3, b3):
        import jax, jax.numpy as jnp
        import numpy as np
        NUM_NODES = 1250
        NUM_EDGES = 20000
        IN_CH = 768
        TYPE_DIM = 128
        HID = 768
        OUT = 768
        NUM_REL = 3
        NUM_NODE_TYPE = 3

        def _glorot(key, shape):
            fan_in, fan_out = (shape[-2], shape[-1])
            lim = (6.0 / (fan_in + fan_out)) ** 0.5
            return jax.random.uniform(key, shape, jnp.float32, -lim, lim)

        def rgcn_conv(h, src, dst, edge_type, w_rel, w_root, bias):
            num_nodes = h.shape[0]
            xw = jnp.einsum('nd,rde->rne', h, w_rel)
            msg = xw[edge_type, src]
            onehot = jax.nn.one_hot(edge_type, NUM_REL, dtype=h.dtype)
            count = jax.ops.segment_sum(onehot, dst, num_segments=num_nodes)
            inv = jnp.where(count > 0, 1.0 / jnp.maximum(count, 1.0), 0.0)
            msg = msg * inv[dst, edge_type][:, None]
            agg = jax.ops.segment_sum(msg, dst, num_segments=num_nodes)
            return agg + h @ w_root + bias
        src, dst = (edge_index[0], edge_index[1])
        h = jnp.concatenate([x, node_emb[node_type]], axis=-1)
        h = jax.nn.relu(rgcn_conv(h, src, dst, edge_type, w_rel1, w_root1, b1))
        h = jax.nn.relu(rgcn_conv(h, src, dst, edge_type, w_rel2, w_root2, b2))
        h = jax.nn.relu(rgcn_conv(h, src, dst, edge_type, w_rel3, w_root3, b3))
        return h
    edge_index = jnp.stack([src, dst])
    h = jnp.maximum(_layernorm(x, axis=-1), 0.0)
    x = x + _L0_gnn_ref(h, edge_index, L0_gnn_norm_g, L0_gnn_norm_b, L0_gnn_W1, L0_gnn_a_src1, L0_gnn_a_dst1, L0_gnn_b1, L0_gnn_W2, L0_gnn_a_src2, L0_gnn_a_dst2, L0_gnn_b2, L0_gnn_Wu, L0_gnn_bu)
    h = jnp.maximum(_layernorm(x, axis=-1), 0.0)
    x = x + _L1_gnn_ref(h, node_type_3, edge_index, edge_type_3, L1_gnn_node_emb, L1_gnn_w_rel1, L1_gnn_w_root1, L1_gnn_b1, L1_gnn_w_rel2, L1_gnn_w_root2, L1_gnn_b2, L1_gnn_w_rel3, L1_gnn_w_root3, L1_gnn_b3)
    return x

_drawn_inputs = setup_inputs


def setup_inputs(seed=0):
    import zlib

    import numpy as np

    out = dict(_drawn_inputs(seed))
    spreads = {'L0_gnn_norm_g': (1.0, 0.6),
     'L0_gnn_norm_b': (0.0, 0.1),
     'L0_gnn_b1': (0.0, 0.1),
     'L0_gnn_b2': (0.0, 0.1),
     'L0_gnn_bu': (0.0, 0.1),
     'L1_gnn_b1': (0.0, 0.1),
     'L1_gnn_b2': (0.0, 0.1),
     'L1_gnn_b3': (0.0, 0.1)}
    factors = {'L0_gnn_a_src1': 4.204, 'L0_gnn_a_dst1': 8.0, 'L0_gnn_a_src2': 8.0, 'L0_gnn_a_dst2': 8.0}
    for name, (base, spread) in spreads.items():
        noise = np.random.default_rng([zlib.crc32(name.encode()), seed]).standard_normal(out[name].shape)
        drawn = base * np.exp(spread * noise) if base else spread * noise
        out[name] = jnp.asarray(drawn.astype(out[name].dtype))
    for name, factor in factors.items():
        out[name] = (out[name] * factor).astype(out[name].dtype)
    return out
```

```python
from contextlib import ExitStack

import concourse.bass as bass
from concourse import mybir

ALU = mybir.AluOpType
ACT = mybir.ActivationFunctionType
AX = mybir.AxisListType
F32 = mybir.dt.float32
F32R = mybir.dt.float32r
BF16 = mybir.dt.bfloat16
I16 = mybir.dt.int16
I32 = mybir.dt.int32

P = 128
EPS = 1e-5
SLOPE = 0.2
NEG = -1e30
TYPE_STEP = 4096
GROUP = 32


def ds(start, size):
    return bass.ds(start, size)


def gnn_kernel(nc, A, out):
    N, D = A["x"].shape
    E = A["src"].shape[0]
    R, D1 = A["w_all1"].shape[0] - 1, A["w_all1"].shape[1]
    TD = A["L1_gnn_node_emb"].shape[1]
    H1, C1 = A["L0_gnn_a_src1"].shape
    H2, C2 = A["L0_gnn_a_src2"].shape
    T = -(-N // P)
    NP = T * P
    LAST = N - (T - 1) * P
    DK = D // P
    ET = -(-E // P)
    EA, EB = P * P, ET - P
    EFULL = E // P - P
    NG = NP // GROUP
    GC = R * GROUP
    QG = P // GROUP
    SB = 512 // GC
    ETP = -(-ET // 2)
    assert SB * 2 >= T and D % P == 0 and T % 2 == 0 and EFULL >= 0

    root = ExitStack()

    def sb(ctx, name, shape, dt):
        return ctx.enter_context(nc.sbuf_tensor(name, shape, dt))

    def pb(ctx, name, shape, dt=F32):
        return ctx.enter_context(nc.psum_tensor(name, shape, dt))

    def sem(ctx, name):
        return ctx.enter_context(nc.semaphore(name))

    counts_dram = nc.dram_tensor("counts_scratch", [R, T, P, T * P], F32, kind="Internal").ap()
    x2_dram = nc.dram_tensor("x2_scratch", [NP, D], F32, kind="Internal").ap()
    arow_dram = [nc.dram_tensor(f"arow_scratch{i}", [H * T, P], F32, kind="Internal").ap()
                 for i, H in enumerate((H1, H2))]
    uvrow_dram = [nc.dram_tensor(f"uvrow_scratch{i}", [2 * H * T, P], F32, kind="Internal").ap()
                  for i, H in enumerate((H1, H2))]

    with root:
        ident = sb(root, "ident", [P, P], F32)
        inv = sb(root, "inv", [P, T, R], F32)
        gat = ExitStack()
        with gat:
            C0 = sb(gat, "C0", [P, T, NP], F32)
            h1e = sb(gat, "h1e", [P, T, H1, C1 + 1], F32)
            with ExitStack() as ctx:
                count_edges(nc, A, ctx, sb, pb, sem, ident, inv, C0, counts_dram, locals())
            with ExitStack() as ctx:
                norm_and_project(nc, A, ctx, sb, pb, sem, ident, h1e, x2_dram, locals())
            neg = sb(gat, "neg", [P, T, NP], BF16)
            out1 = sb(gat, "out1", [P, T, D], F32)
            with ExitStack() as ctx:
                gat_attention(nc, A, ctx, sb, pb, sem, ident, C0, neg, h1e, out1, H1, C1, "1",
                              arow_dram[0], uvrow_dram[0], True, locals())
            h2e = sb(gat, "h2e", [P, T, H2, C2 + 1], F32)
            with ExitStack() as ctx:
                project2(nc, A, ctx, sb, pb, sem, ident, out1, h2e, locals())
            out2 = out1[:, :, 0:H2 * C2]
            with ExitStack() as ctx:
                gat_attention(nc, A, ctx, sb, pb, sem, ident, C0, neg, h2e, out2, H2, C2, "2",
                              arow_dram[1], uvrow_dram[1], False, locals())
            with ExitStack() as ctx:
                update_x(nc, A, ctx, sb, pb, sem, ident, out2, x2_dram, locals())
        with ExitStack() as ctx:
            rgcn(nc, A, ctx, sb, pb, sem, ident, inv, x2_dram, counts_dram, out, locals())


def count_edges(nc, A, ctx, sb, pb, sem, ident, inv, C0, counts_dram, dims):
    T, NP, ET, EA, EB, EFULL = (dims[k] for k in ("T", "NP", "ET", "EA", "EB", "EFULL"))
    NG, GC, QG, SB, ETP, R, E = (dims[k] for k in ("NG", "GC", "QG", "SB", "ETP", "R", "E"))
    PAIR = 2 * QG

    raw = sb(ctx, "edges_raw", [P, 3, 2, P], I32)
    edges = sb(ctx, "edges_f", [P, 3, 2, P], F32)
    key = sb(ctx, "edge_key", [P, 2, P], F32)
    src_col = sb(ctx, "src_col", [P, 2 * P], F32)
    key_col = sb(ctx, "key_col", [P, 2 * P], F32)
    iota_src = sb(ctx, "iota_src", [P, NP], I16)
    iota_key = sb(ctx, "iota_key", [P, NG * GC], I16)
    ones = sb(ctx, "count_ones", [P, P], F32)
    ones_r = sb(ctx, "count_ones_r", [P, 2], F32R)
    span = sb(ctx, "tile_span", [P, 2, 2], F32)
    span_b = sb(ctx, "tile_span_b", [P, 2, 2, NG], F32)
    jcol = sb(ctx, "jcol", [NG, ETP], F32)
    gcol = sb(ctx, "gcol", [NG, 2], F32)
    tri = sb(ctx, "tri", [NG, NG], F32)
    pair_span = sb(ctx, "pair_span", [NG, 2, ETP], F32)
    hit = sb(ctx, "hit", [NG, 3, ETP], F32)
    rng = sb(ctx, "rng", [NG, 6], F32)
    table = sb(ctx, "table", [1, 2 * NG], I32)
    hot_src = sb(ctx, "hot_src", [P, 2, NP], BF16)
    hot_key = sb(ctx, "hot_key", [P, 2, GC], BF16)
    stage = [sb(ctx, f"count_stage{i}", [P, R, T, P], F32R) for i in range(2)]
    zero_b = sb(ctx, "zero_b", [P, 512], BF16)

    cnt_ps = [[pb(ctx, f"cnt_ps{i}{b}", [P, 512]) for b in range(2)] for i in range(2)]
    misc = pb(ctx, "misc_ps", [P, 512])
    deg = pb(ctx, "deg_ps", [P, 512])

    s_pad, s_load, s_edge_f, s_const = (sem(ctx, n) for n in ("pad_set", "edges_in", "edges_conv", "consts"))
    s_tr, s_cols, s_dve, s_bc, s_pre, s_row, s_table = (sem(ctx, n) for n in (
        "edges_turned", "cols_ready", "dve_step", "span_bc", "visits_summed", "row_ready", "table_ready"))
    s_free, s_hot, s_group, s_copied = (sem(ctx, n) for n in ("slot_free", "hot_ready", "group_done", "group_copied"))
    s_deg, s_inv, s_c0, s_bank = (sem(ctx, n) for n in ("degrees", "inv_done", "c0_tile_done", "bank_free"))
    s_out = [sem(ctx, f"counts_stored{i}") for i in range(2)]
    s_spanb = sem(ctx, "span_copied")

    def ranges(eng):
        def read(g):
            span = eng.value_load(table[0:1, ds(g, 1)], min_val=0, max_val=(ETP - 1) * P + ETP)
            shift = eng.value_load(table[0:1, ds(g + NG, 1)], min_val=0, max_val=(NG + 1) * ETP)
            return span // P, span % P, shift
        return read

    with nc.Block() as block:
        @block.sync
        def _(sp):
            sp.wait_ge(s_pad, 1)
            for i, name in enumerate(("src", "dst", "edge_type_3")):
                a = A[name]
                sp.dma_start(raw[:, i, 0, :], a[0:EA].rearrange("(j p) -> j p", p=P)).then_inc(s_load, 16)
                if EFULL:
                    sp.dma_start(raw[0:EFULL, i, 1, :],
                                 a[EA:EA + EFULL * P].rearrange("(j p) -> j p", p=P)).then_inc(s_load, 16)
                if EB > EFULL:
                    rest = E - EA - EFULL * P
                    sp.dma_start(raw[EFULL:EB, i, 1, 0:rest],
                                 a[EA + EFULL * P:E].rearrange("(j p) -> j p", j=1)).then_inc(s_load, 16)
            for half in range(2):
                sp.sem_inc(s_out[half], 16 * R)
            with sp.Fori(0, T // 2) as t2:
                for half in range(2):
                    sp.wait_ge(s_copied, PAIR * t2 + QG * (half + 1) + 2)
                    for r in range(R):
                        sp.dma_start(counts_dram[r, ds(2 * t2 + half, 1)].rearrange("o p n -> (o p) n"),
                                     stage[half][:, r].rearrange("p t d -> p (t d)").bitcast(F32)).then_inc(s_out[half], 16)
            for half in range(2):
                sp.wait_ge(s_out[half], 16 * R * (T // 2 + 1))

        @block.gpsimd
        def _(pool):
            pool.memset(ones[:], 1.0).then_inc(s_const, 1)
            pool.memset(zero_b[:], 0.0).then_inc(s_const, 1)
            pool.iota(iota_src[:], [[1, NP]], base=0, channel_multiplier=0,
                      allow_small_or_imprecise_dtypes=True).then_inc(s_const, 1)
            pool.iota(iota_key[:].rearrange("p (g r i) -> p g r i", g=NG, r=R),
                      [[GROUP, NG], [TYPE_STEP, R], [1, GROUP]], base=0, channel_multiplier=0,
                      allow_small_or_imprecise_dtypes=True).then_inc(s_const, 1)
            pool.iota(jcol[:], [[1, ETP]], base=0, channel_multiplier=0,
                      allow_small_or_imprecise_dtypes=True).then_inc(s_const, 1)
            pool.iota(gcol[:], [[GROUP - 1, 2]], base=0, channel_multiplier=GROUP,
                      allow_small_or_imprecise_dtypes=True).then_inc(s_const, 1)
            pool.wait_ge(s_const, 1)
            pool.affine_select(out=ident[:], in_=ones[:], compare_op=ALU.is_equal, fill=0.0, base=0,
                               pattern=[[-1, P]], channel_multiplier=1).then_inc(s_const, 1)
            pool.affine_select(out=tri[:], in_=ones[0:NG, 0:NG], compare_op=ALU.is_ge, fill=0.0, base=-1,
                               pattern=[[1, NG]], channel_multiplier=-1).then_inc(s_const, 1)

        N_CONST = 8

        @block.vector
        def _(dve):
            nc.vector.memset(raw[:, 0, 1, :], -1)
            nc.vector.memset(raw[:, 1, 1, :], NP - 1)
            nc.vector.memset(raw[:, 2, 1, :], 0).then_inc(s_pad, 1)
            dve.wait_ge(s_load, 16 * 3 * (1 + (EFULL > 0) + (EB > EFULL)))
            step = 0
            nc.vector.tensor_copy(edges[:], raw[:]).then_inc(s_dve, 1)
            step += 1
            dve.wait_ge(s_dve, step)
            nc.vector.scalar_tensor_tensor(key[:], edges[:, 2], float(TYPE_STEP), edges[:, 1],
                                           ALU.mult, ALU.add).then_inc(s_edge_f, 1)
            nc.vector.tensor_reduce(span[:, :, 0:1], edges[:, 1], AX.X, ALU.min)
            nc.vector.tensor_reduce(span[:, :, 1:2], edges[:, 1], AX.X, ALU.max).then_inc(s_dve, 1)
            step += 1
            dve.wait_ge(s_dve, step)
            dve.wait_ge(s_const, N_CONST)
            for half in range(2):
                for m in range(2):
                    last = nc.vector.tensor_scalar(span_b[:, half, m, :], ones[:, 0:NG],
                                                   span[:, half, m:m + 1], None, ALU.mult)
            last.then_inc(s_spanb, 1)
            dve.wait_ge(s_tr, 1)
            nc.vector.tensor_copy(src_col[:], misc[:, 0:2 * P])
            nc.vector.tensor_copy(ones_r[:], ones[:, 0:2])
            nc.vector.tensor_copy(key_col[:], misc[:, 2 * P:4 * P]).then_inc(s_cols, 1)
            dve.wait_ge(s_bc, 1)
            for m, op in enumerate((ALU.min, ALU.max)):
                last = nc.vector.tensor_reduce(
                    pair_span[:, m, :], deg[0:NG, 256 * m:256 * m + 2 * ETP].rearrange("g (j two) -> g j two", two=2),
                    AX.X, op)
            last.then_inc(s_dve, 1)
            step += 1
            dve.wait_ge(s_dve, step)
            nc.vector.tensor_scalar(hit[:, 0], pair_span[:, 0], gcol[:, 1:2], None, ALU.is_le).then_inc(s_dve, 1)
            step += 1
            dve.wait_ge(s_dve, step)
            nc.vector.scalar_tensor_tensor(hit[:, 1], pair_span[:, 1], gcol[:, 0:1], hit[:, 0],
                                           ALU.is_ge, ALU.mult).then_inc(s_dve, 1)
            step += 1
            dve.wait_ge(s_dve, step)
            nc.vector.scalar_tensor_tensor(hit[:, 0], jcol[:], 1.0, hit[:, 1], ALU.add, ALU.mult)
            nc.vector.tensor_scalar(hit[:, 2], jcol[:], -1.0, float(2 * P), ALU.mult, ALU.add).then_inc(s_dve, 1)
            step += 1
            dve.wait_ge(s_dve, step)
            nc.vector.tensor_tensor(hit[:, 2], hit[:, 2], hit[:, 1], ALU.mult).then_inc(s_dve, 1)
            step += 1
            dve.wait_ge(s_dve, step)
            nc.vector.tensor_reduce(rng[:, 3:4], hit[:, 0], AX.X, ALU.max)
            nc.vector.tensor_reduce(rng[:, 4:5], hit[:, 2], AX.X, ALU.max).then_inc(s_dve, 1)
            step += 1
            dve.wait_ge(s_dve, step)
            nc.vector.tensor_scalar(rng[:, 1:2], rng[:, 3:4], 1.0, None, ALU.max).then_inc(s_dve, 1)
            nc.vector.tensor_scalar(rng[:, 5:6], rng[:, 4:5], -1.0, float(2 * P), ALU.mult, ALU.add).then_inc(s_dve, 1)
            step += 2
            dve.wait_ge(s_dve, step)
            nc.vector.scalar_tensor_tensor(rng[:, 0:1], rng[:, 1:2], -1.0, rng[:, 5:6],
                                           ALU.add, ALU.min).then_inc(s_dve, 1)
            step += 1
            dve.wait_ge(s_dve, step)
            nc.vector.tensor_tensor(rng[:, 3:4], rng[:, 1:2], rng[:, 0:1], ALU.subtract)
            nc.vector.tensor_scalar(rng[:, 4:5], rng[:, 0:1], -1.0, None, ALU.mult)
            nc.vector.scalar_tensor_tensor(rng[:, 2:3], rng[:, 0:1], float(P), rng[:, 1:2], ALU.mult,
                                           ALU.add).then_inc(s_row, 1)
            dve.wait_ge(s_pre, 1)
            nc.vector.tensor_copy(table[:, 0:NG], misc[0:1, 0:NG])
            nc.vector.tensor_scalar(table[:, NG:2 * NG], misc[0:1, NG:2 * NG], float(ETP), None,
                                    ALU.add).then_inc(s_table, 1)
            dve.sem_inc(s_c0, 2)
            dve.sem_inc(s_inv, 1)
            dve.wait_ge(s_table, 1)
            dve.sem_inc(s_hot, 2 * ETP)
            read = ranges(dve)
            with dve.Fori(0, T // 2) as t2:
                for q in range(PAIR):
                    lo, end, shift = read(PAIR * t2 + q)
                    with dve.Fori(lo, end) as j:
                        v = j + shift
                        for tile in range(2):
                            dve.wait_ge(s_free, 2 * v + tile + 1)
                            nc.vector.tensor_scalar(hot_src[:, tile], iota_src[:],
                                                    src_col[:, ds(2 * j + tile, 1)], None, ALU.is_equal)
                            nc.vector.tensor_scalar(hot_key[:, tile], iota_key[:, ds((PAIR * t2 + q) * GC, GC)],
                                                    key_col[:, ds(2 * j + tile, 1)], None,
                                                    ALU.is_equal).then_inc(s_hot, 1)
                    if q % QG == QG - 1:
                        half = q // QG
                        t = 2 * t2 + half
                        dve.wait_ge(s_copied, PAIR * t2 + QG * (half + 1) + 2)
                        cols = C0[:, :, ds(t * P, P)]
                        st = stage[half]
                        nc.vector.tensor_tensor(cols, st[:, 0].bitcast(F32), st[:, 1].bitcast(F32), ALU.add)
                        dve.drain()
                        nc.vector.tensor_tensor(cols, cols, st[:, 2].bitcast(F32), ALU.add)
                        dve.drain()
                        diag = C0[:, ds(t, 1), ds(t * P, P)].rearrange("p o d -> p (o d)")
                        nc.vector.tensor_tensor(diag, diag, ident[:], ALU.add).then_inc(s_c0, 1)
                        dve.wait_ge(s_deg, 2 * t2 + half + 3)
                        nc.vector.tensor_scalar(inv[:, ds(t, 1), :].rearrange("p o r -> p (o r)"),
                                                deg[:, 0:2 * R:2], 1.0, None, ALU.max)
                        dve.drain()
                        flat = inv[:, ds(t, 1), :].rearrange("p o r -> p (o r)")
                        nc.vector.reciprocal(flat, flat).then_inc(s_inv, 1)

        @block.scalar
        def _(act):
            act.sem_inc(s_copied, 2)
            with act.Fori(0, T // 2) as t2:
                for q in range(PAIR):
                    half, part = q // QG, q % QG
                    act.wait_ge(s_group, PAIR * t2 + q + 1)
                    if part == 0:
                        act.wait_ge(s_c0, 2 * t2 + half + 1)
                        act.wait_ge(s_deg, 2 * t2 + half + 1)
                        act.wait_ge(s_out[half], 16 * R * (t2 + 1))
                    for b in range(2):
                        n = min(SB, T - b * SB)
                        ins = nc.scalar.copy(
                            stage[half][:, :, b * SB:b * SB + n, part * GROUP:(part + 1) * GROUP]
                            .rearrange("p r t i -> p t r i"),
                            cnt_ps[q % 2][b][:, 0:n * GC].rearrange("p (t r i) -> p t r i", t=n, r=R))
                    ins.then_inc(s_copied, 1)

        @block.tensor
        def _(pe):
            pe.wait_ge(s_edge_f, 1)
            pe.wait_ge(s_const, N_CONST)
            for half in range(2):
                nc.tensor.transpose(misc[:, half * P:(half + 1) * P], edges[:, 0, half], ident[:])
                last = nc.tensor.transpose(misc[:, (2 + half) * P:(3 + half) * P], key[:, half], ident[:])
            last.then_inc(s_tr, 1)
            pe.wait_ge(s_spanb, 1)
            for m in range(2):
                nc.tensor.matmul(deg[0:NG, 256 * m:256 * m + P], span_b[:, 0, m, :], ident[:], start=True, stop=True)
                last = nc.tensor.matmul(deg[0:NG, 256 * m + P:256 * m + 2 * ETP], span_b[:, 1, m, :],
                                        ident[:, 0:2 * ETP - P],
                                        start=True, stop=True)
            last.then_inc(s_bc, 1)
            pe.wait_ge(s_row, 1)
            pe.wait_ge(s_cols, 1)
            nc.tensor.matmul(misc[0:1, 0:NG], rng[:, 2:3], ident[0:NG, 0:NG], start=True, stop=True)
            nc.tensor.matmul(misc[0:1, NG:2 * NG], rng[:, 3:4], tri[:], start=True, stop=False)
            nc.tensor.matmul(misc[0:1, NG:2 * NG], rng[:, 4:5], ident[0:NG, 0:NG], start=False,
                             stop=True).then_inc(s_pre, 1)
            pe.sem_inc(s_free, 2 * ETP + 2)
            pe.sem_inc(s_deg, 2)
            pe.wait_ge(s_table, 1)
            read = ranges(pe)
            with pe.Fori(0, T // 2) as t2:
                for q in range(PAIR):
                    bank = cnt_ps[q % 2]
                    pe.wait_ge(s_copied, PAIR * t2 + q + 1)
                    for b in range(2):
                        nc.tensor.matmul(bank[b][:, 0:min(SB, T - b * SB) * GC], zero_b[:, 0:P],
                                         zero_b[:, 0:min(SB, T - b * SB) * GC], start=True, stop=False,
                                         skip_group_check=True)
                    lo, end, shift = read(PAIR * t2 + q)
                    with pe.Fori(lo, end) as j:
                        v = j + shift
                        for tile in range(2):
                            pe.wait_ge(s_hot, 2 * v + tile + 1)
                            for s in range(T):
                                b, c = s // SB, s % SB
                                last = nc.tensor.matmul(bank[b][:, c * GC:(c + 1) * GC],
                                                        hot_src[:, tile, s * P:(s + 1) * P], hot_key[:, tile],
                                                        start=False, stop=True, skip_group_check=True)
                            last.then_inc(s_free, 1)
                    pe.matmul(misc[:, 0:2], zero_b[:, 0:P], zero_b[:, 0:2], start=True, stop=True,
                              skip_group_check=True).then_inc(s_group, 1)
                    if q % QG == QG - 1:
                        half = q // QG
                        pe.wait_ge(s_copied, PAIR * t2 + QG * (half + 1) + 2)
                        pe.wait_ge(s_inv, 2 * t2 + half + 1)
                        for r in range(R):
                            for s in range(T):
                                last = nc.tensor.matmul(deg[:, 2 * r:2 * r + 2], stage[half][:, r, s, :], ones_r[:],
                                                        start=(s == 0), stop=(s == T - 1))
                        last.then_inc(s_deg, 1)


def norm_and_project(nc, A, ctx, sb, pb, sem, ident, h1e, x2_dram, dims):
    T, D, DK, H1, C1, LAST = (dims[k] for k in ("T", "D", "DK", "H1", "C1", "LAST"))
    HALF = D // 2
    HH = H1 // 2
    x = sb(ctx, "x", [P, T, D], F32)
    w1 = sb(ctx, "w1", [P, DK, D], F32)
    wu = sb(ctx, "wu", [P, DK, D], F32)
    gb = sb(ctx, "norm_gb", [P, 2, DK], F32)
    bu = sb(ctx, "bu", [P, D], F32)
    eps = sb(ctx, "eps", [P, 1], F32)
    h = [sb(ctx, f"h{i}", [P, D], F32) for i in range(2)]
    xhat = [sb(ctx, f"xhat{i}", [P, D], F32) for i in range(2)]
    hT = [sb(ctx, f"hT{i}", [P, DK, P], F32) for i in range(2)]
    xT = [sb(ctx, f"xT{i}", [P, DK, P], F32) for i in range(2)]
    x2 = [sb(ctx, f"x2_{i}", [P, D], F32) for i in range(2)]
    st = sb(ctx, "bn", [P, 2, 2, 2, 6], F32)
    mv = sb(ctx, "mean_var", [P, 2, 2, 6], F32)
    turn = pb(ctx, "turn_ps", [P, 2, 1024])
    y = pb(ctx, "y_ps", [P, 2, 512])
    hp = pb(ctx, "h1_ps", [P, 2, 512])

    s_x = [sem(ctx, f"x_in{i}") for i in range(2)]
    s_w, s_gb, s_eps, s_seen = (sem(ctx, n) for n in ("w_in", "gb_in", "eps_set", "statistics_seen"))
    s_part = sem(ctx, "x_plus_hwu")
    s_d, s_var, s_sd, s_aff, s_h, s_xhat = (sem(ctx, n) for n in (
        "dve_step", "var_ready", "sd_ready", "affine_ready", "h_ready", "xhat_ready"))
    s_turn, s_hT, s_xT, s_y, s_h1p, s_h1, s_x2, = (sem(ctx, n) for n in (
        "turned", "hT_ready", "xT_ready", "y_done", "h1_done", "h1_copied", "x2_ready"))
    s_st = [sem(ctx, f"x2_stored{i}") for i in range(2)]

    with nc.Block() as block:
        @block.sync
        def _(sp):
            sp.wait_ge(s_eps, 2)
            sp.dma_start(x[:, 0:2, :], A["x"][0:2 * P].rearrange("(t p) d -> p t d", p=P)).then_inc(s_x[0], 16)
            sp.dma_start(x[:, 2:T - 1, :],
                         A["x"][2 * P:(T - 1) * P].rearrange("(t p) d -> p t d", p=P)).then_inc(s_x[1], 16)
            sp.dma_start(x[0:LAST, T - 1, :], A["x"][(T - 1) * P:]).then_inc(s_x[1], 16)
            sp.dma_start(wu[:], A["L0_gnn_Wu"][0:D].rearrange("(k p) n -> p k n", p=P)).then_inc(s_w, 16)
            sp.dma_start(bu[:], A["L0_gnn_bu"].rearrange("(a d) -> a d", a=1).to_broadcast([P, D])).then_inc(s_w, 16)
            with nc.allow_non_contiguous_dma(reason="two vectors of one column per feature tile"):
                sp.dma_start(gb[:, 0, :], A["L0_gnn_norm_g"].rearrange("(k p) -> p k", p=P)).then_inc(s_gb, 16)
                sp.dma_start(gb[:, 1, :], A["L0_gnn_norm_b"].rearrange("(k p) -> p k", p=P)).then_inc(s_gb, 16)
            sp.dma_start(w1[:], A["L0_gnn_W1"].rearrange("(k p) n -> p k n", p=P)).then_inc(s_gb, 16)
            for i in range(2):
                sp.sem_inc(s_st[i], 16)
            with sp.Fori(0, T // 2) as t2:
                for i in range(2):
                    sp.wait_ge(s_x2, 2 * t2 + i + 2)
                    sp.dma_start(x2_dram[ds((2 * t2 + i) * P, P), :], x2[i][:]).then_inc(s_st[i], 16)
            for i in range(2):
                sp.wait_ge(s_st[i], 16 * (T // 2 + 1))

        @block.gpsimd
        def _(pool):
            pool.memset(x[:, T - 1, :], 0.0).then_inc(s_eps, 1)
            pool.memset(eps[:], EPS).then_inc(s_eps, 1)
            pool.memset(h1e[:, :, :, C1:C1 + 1], 1.0).then_inc(s_eps, 1)

        def steps(t2, i):
            return 2 * t2 + i

        @block.vector
        def _(dve):
            dve.wait_ge(s_x[0], 16)
            dve.wait_ge(s_x[1], 32)
            dve.wait_ge(s_w, 32)
            def norm(t, i, w, src):
                base = 4 * t + 2 * w
                m = mv[:, i, w, :]
                for c in range(2):
                    last = nc.vector.bn_stats(st[:, i, w, c, :], src[:, c * HALF:(c + 1) * HALF])
                last.then_inc(s_d, 1)
                dve.wait_ge(s_d, base + 1)
                dve.sem_inc(s_seen, 1)
                nc.vector.bn_aggr(m[:, 0:2], st[:, i, w].rearrange("p c s -> p (c s)")).then_inc(s_var, 1)
                dve.wait_ge(s_sd, 2 * t + w + 1)
                nc.vector.reciprocal(m[:, 3:4], m[:, 2:3]).then_inc(s_d, 1)
                dve.wait_ge(s_d, base + 2)
                nc.vector.scalar_tensor_tensor(m[:, 4:5], m[:, 0:1], -1.0, m[:, 3:4], ALU.mult,
                                               ALU.mult).then_inc(s_aff, 1)

            def front(t, i):
                norm(t, i, 0, x[:, ds(t, 1), :].rearrange("p o d -> p (o d)"))
                dve.wait_ge(s_h, t + 1)
                norm(t, i, 1, h[i])
                nc.vector.tensor_scalar(xhat[i][:], h[i][:], mv[:, i, 1, 0:1], mv[:, i, 1, 3:4],
                                        ALU.subtract, ALU.mult).then_inc(s_xhat, 1)

            def back(t, i, t2):
                xt = x[:, ds(t, 1), :].rearrange("p o d -> p (o d)")
                dve.wait_ge(s_y, t + 1)
                dve.wait_ge(s_st[i], 16 * (t2 + 1))
                nc.vector.tensor_tensor(x2[i][:].rearrange("p (c n) -> p c n", c=2), y[:, :, 0:HALF],
                                        xt.rearrange("p (c n) -> p c n", c=2), ALU.add).then_inc(s_part, 1)
                dve.wait_ge(s_part, t + 1)
                nc.vector.tensor_tensor(x2[i][:], x2[i][:], bu[:], ALU.add).then_inc(s_x2, 1)

            front(0, 0)
            with dve.Fori(0, T // 2 - 1) as t2:
                for i in range(2):
                    front(2 * t2 + i + 1, 1 - i)
                    back(2 * t2 + i, i, t2)
            front(T - 1, 1)
            for i in range(2):
                back(T - 2 + i, i, T // 2 - 1)

        @block.scalar
        def _(act):
            act.wait_ge(s_eps, 2)
            act.wait_ge(s_gb, 48)
            def front(t, i):
                xt = x[:, ds(t, 1), :].rearrange("p o d -> p (o d)")
                act.wait_ge(s_var, 2 * t + 1)
                nc.scalar.activation(mv[:, i, 0, 2:3], mv[:, i, 0, 1:2], ACT.Sqrt, bias=eps[:]).then_inc(s_sd, 1)
                act.wait_ge(s_aff, 2 * t + 1)
                nc.scalar.activation(h[i][:], xt, ACT.Relu, bias=mv[:, i, 0, 4:5],
                                     scale=mv[:, i, 0, 3:4]).then_inc(s_h, 1)
                act.wait_ge(s_var, 2 * t + 2)
                nc.scalar.activation(mv[:, i, 1, 2:3], mv[:, i, 1, 1:2], ACT.Sqrt, bias=eps[:]).then_inc(s_sd, 1)

            def back(t, i, following=None):
                act.wait_ge(s_turn, 2 * t + 1)
                nc.scalar.copy(hT[i][:].rearrange("p k n -> p (k n)"), turn[:, 0, 0:D]).then_inc(s_hT, 1)
                act.wait_ge(s_turn, 2 * t + 2)
                for k in range(DK):
                    last = nc.scalar.activation(xT[i][:, k, :], turn[:, 1, k * P:(k + 1) * P], ACT.Identity,
                                                bias=gb[:, 1, k:k + 1], scale=gb[:, 0, k:k + 1])
                last.then_inc(s_xT, 1)
                if following:
                    front(*following)
                act.wait_ge(s_h1p, t + 1)
                dst = h1e[:, ds(t, 1), :, 0:C1].rearrange("p o h c -> p (o h) c")
                for c in range(2):
                    last = nc.scalar.copy(dst[:, c * HH:(c + 1) * HH, :],
                                          hp[:, c, 0:HALF].rearrange("p (h c) -> p h c", h=HH))
                last.then_inc(s_h1, 1)

            front(0, 0)
            with act.Fori(0, T // 2 - 1) as t2:
                for i in range(2):
                    back(2 * t2 + i, i, (2 * t2 + i + 1, 1 - i))
            back(T - 2, 0, (T - 1, 1))
            back(T - 1, 1)

        @block.tensor
        def _(pe):
            pe.wait_ge(s_w, 32)
            pe.wait_ge(s_gb, 48)
            pe.sem_inc(s_h1, 1)
            pe.sem_inc(s_x2, 1)
            with pe.Fori(0, T // 2) as t2:
                for i in range(2):
                    t = 2 * t2 + i
                    pe.wait_ge(s_h, t + 1)
                    for k in range(DK):
                        last = nc.tensor.transpose(turn[:, 0, k * P:(k + 1) * P], h[i][:, k * P:(k + 1) * P], ident[:])
                    last.then_inc(s_turn, 1)
                    pe.wait_ge(s_xhat, t + 1)
                    for k in range(DK):
                        last = nc.tensor.transpose(turn[:, 1, k * P:(k + 1) * P], xhat[i][:, k * P:(k + 1) * P], ident[:])
                    last.then_inc(s_turn, 1)
                    pe.wait_ge(s_hT, t + 1)
                    pe.wait_ge(s_x2, t + 1)
                    for k in range(DK):
                        for c in range(2):
                            last = nc.tensor.matmul(y[:, c, 0:HALF], hT[i][:, k, :], wu[:, k, c * HALF:(c + 1) * HALF],
                                                    start=(k == 0), stop=(k == DK - 1))
                    last.then_inc(s_y, 1)
                    pe.wait_ge(s_xT, t + 1)
                    pe.wait_ge(s_h1, t + 1)
                    for k in range(DK):
                        for c in range(2):
                            last = nc.tensor.matmul(hp[:, c, 0:HALF], xT[i][:, k, :], w1[:, k, c * HALF:(c + 1) * HALF],
                                                    start=(k == 0), stop=(k == DK - 1))
                    last.then_inc(s_h1p, 1)


def gat_attention(nc, A, ctx, sb, pb, sem, ident, C0, neg, he, o, H, C, n, arow_dram, uvrow_dram, make_neg, dims):
    T, NP = dims["T"], dims["NP"]
    HT = H * T
    W = 5
    a_bc = sb(ctx, f"a_bc{n}", [P, 2, H, C], F32)
    b_bc = sb(ctx, f"b_bc{n}", [P, H, C], F32)
    sc = sb(ctx, f"scores{n}", [P, 2, H, T], F32)
    sc2 = sb(ctx, f"scores_leaky{n}", [P, H, T], F32)
    top = sb(ctx, f"top{n}", [P, H, T], F32)
    mx = sb(ctx, f"mx{n}", [P, H, T], F32)
    uv = sb(ctx, f"uv{n}", [P, H, 2, T], F32)
    arow = sb(ctx, f"arow{n}", [HT, P], F32)
    uvrow = sb(ctx, f"uvrow{n}", [2 * T, H, P], F32)
    big = sb(ctx, f"s_src_bc{n}", [P, W, NP], F32)
    uv_bc = [sb(ctx, f"uv_bc{n}{i}", [P, 2, NP], F32) for i in range(2)]
    rden = sb(ctx, f"rden{n}", [P, T], F32)
    junk = sb(ctx, f"junk{n}", [P, 2, NP], F32)
    acc = pb(ctx, f"acc{n}", [P, T, 256])
    tp = pb(ctx, f"turn{n}", [P, 1536])

    s_ab, s_junk, s_tr, s_row, s_rst, s_abc = (sem(ctx, f"{x}{n}") for x in (
        "ab_in", "reduced", "rows_turned", "rows_copied", "rows_stored", "s_src_bc_in"))
    s_ct, s_neg, s_d, s_uv = (sem(ctx, f"{x}{n}") for x in ("c0_turned", "neg_done", "dve_step", "uv_done"))
    s_uvin = [sem(ctx, f"uv_in{n}{i}") for i in range(2)]
    s_lin, s_z, s_e, s_w, s_used, s_o = (sem(ctx, f"{x}{n}") for x in (
        "linear_done", "z_done", "exp_done", "weight_done", "weight_used", "head_out"))
    assert H < W and 2 * HT <= P and T % W == 0

    with nc.Block() as block:
        @block.sync
        def _(sp):
            for i, name in enumerate(("src", "dst")):
                sp.dma_start(a_bc[:, i].rearrange("p h c -> p (h c)"),
                             A[f"L0_gnn_a_{name}{n}"].rearrange("(a h) c -> a (h c)", a=1)
                             .to_broadcast([P, H * C])).then_inc(s_ab, 16)
            sp.dma_start(b_bc[:].rearrange("p h c -> p (h c)"),
                         A[f"L0_gnn_b{n}"].rearrange("(a d) -> a d", a=1).to_broadcast([P, H * C])).then_inc(s_ab, 16)
            sp.wait_ge(s_row, 1)
            sp.dma_start(arow_dram, arow[:]).then_inc(s_rst, 16)
            sp.wait_ge(s_rst, 16)
            sp.dma_start(big[:, 0:H, :].rearrange("p h n -> p (h n)"),
                         arow_dram.rearrange("(a r) p -> a (r p)", a=1).to_broadcast([P, HT * P])).then_inc(s_abc, 16)
            rows = uvrow_dram.rearrange("(h r) p -> h (r p)", h=H)
            for h in range(H):
                sp.wait_ge(s_row, 2 + h)
                sp.dma_start(uvrow_dram[2 * T * h:2 * T * (h + 1)], uvrow[:, h]).then_inc(s_rst, 16)
                sp.wait_ge(s_rst, 16 * (h + 2))
                if h >= 2:
                    sp.wait_ge(s_z, T * (h - 1))
                sp.dma_start(uv_bc[h % 2][:].rearrange("p w n -> p (w n)"),
                             rows[h:h + 1].to_broadcast([P, 2 * NP])).then_inc(s_uvin[h % 2], 16)

        @block.vector
        def _(dve):
            dve.wait_ge(s_ab, 48)
            reductions = 0

            def reduce_product(size, in0, in1, start, op0, op1, to):
                nonlocal reductions
                if reductions >= 2:
                    dve.wait_ge(s_junk, reductions - 1)
                nc.vector.tensor_tensor_reduce(junk[:, reductions % 2, 0:size], in0, in1, 1.0, start, op0, op1,
                                               to).then_inc(s_junk, 1)
                reductions += 1

            for i in range(2):
                for h in range(H):
                    for t in range(T):
                        reduce_product(C, he[:, t, h, 0:C], a_bc[:, i, h, :], 0.0, ALU.mult, ALU.add,
                                       sc[:, i, h, t:t + 1])
            if make_neg:
                for t in range(T):
                    dve.wait_ge(s_ct, t + 1)
                    nc.vector.tensor_scalar(neg[:, t, :], tp[:, 0:NP], 0.0, NEG, ALU.is_equal,
                                            ALU.mult).then_inc(s_neg, 1)
                dve.wait_ge(s_neg, T)
            dve.wait_ge(s_junk, reductions)
            nc.vector.tensor_scalar(sc2[:], sc[:, 0], SLOPE, None, ALU.mult)
            dve.wait_ge(s_abc, 16)
            for h in range(H):
                for t in range(T):
                    reduce_product(NP, neg[:, t, :], big[:, h, :], -3e38, ALU.add, ALU.max, top[:, h, t:t + 1])
                dve.wait_ge(s_junk, reductions)
                nc.vector.tensor_tensor(top[:, h], top[:, h], sc[:, 1, h], ALU.add).then_inc(s_d, 1)
                dve.wait_ge(s_d, 2 * h + 1)
                nc.vector.scalar_tensor_tensor(mx[:, h], top[:, h], SLOPE, top[:, h], ALU.mult,
                                               ALU.max).then_inc(s_d, 1)
                dve.wait_ge(s_d, 2 * h + 2)
                nc.vector.tensor_tensor(uv[:, h, 0], sc[:, 1, h], mx[:, h], ALU.subtract)
                nc.vector.scalar_tensor_tensor(uv[:, h, 1], sc[:, 1, h], SLOPE, mx[:, h], ALU.mult,
                                               ALU.subtract).then_inc(s_uv, 1)

            def exponent(i):
                h, k = i // T, i % T
                if k == 0:
                    dve.wait_ge(s_uvin[h % 2], 16 * (h // 2 + 1))
                dve.wait_ge(s_lin, i + 1)
                nc.vector.scalar_tensor_tensor(big[:, i % W], uv_bc[h % 2][:, 0], sc[:, 0, h, k:k + 1],
                                               big[:, i % W], ALU.add, ALU.max).then_inc(s_z, 1)

            def take(h):
                dve.wait_ge(s_used, T * (h + 1))
                nc.vector.reciprocal(rden[:], acc[:, :, C:C + 1].rearrange("p t o -> p (t o)")).then_inc(s_d, 1)
                dve.wait_ge(s_d, 2 * H + 1 + h)
                for t in range(T):
                    nc.vector.scalar_tensor_tensor(o[:, t, h * C:(h + 1) * C], acc[:, t, 0:C], rden[:, t:t + 1],
                                                   b_bc[:, h], ALU.mult, ALU.add).then_inc(s_o, 1)

            exponent(0)
            for i in range(HT):
                if i + 1 < HT:
                    exponent(i + 1)
                dve.wait_ge(s_e, i + 1)
                nc.vector.scalar_tensor_tensor(big[:, i % W], big[:, i % W], 1.0, C0[:, i % T], ALU.min,
                                               ALU.mult).then_inc(s_w, 1)
                if i % T == 1 and i > T:
                    take(i // T - 1)
            take(H - 1)

        @block.scalar
        def _(act):
            act.wait_ge(s_tr, 1)
            nc.scalar.copy(arow[:], acc[0:HT, 0, 0:P]).then_inc(s_row, 1)
            for h in range(H):
                act.wait_ge(s_tr, 2 + h)
                nc.scalar.copy(uvrow[:, h], tp[0:2 * T, 512 * (h % 2):512 * (h % 2) + P]).then_inc(s_row, 1)
            act.wait_ge(s_uv, H)

            def linear(i):
                h, k = i // T, i % T
                if k == 0:
                    act.wait_ge(s_uvin[h % 2], 16 * (h // 2 + 1))
                if i >= W:
                    act.wait_ge(s_used, i - W + 1)
                nc.scalar.activation(big[:, i % W], uv_bc[h % 2][:, 1], ACT.Identity,
                                     bias=sc2[:, h, k:k + 1]).then_inc(s_lin, 1)

            linear(0)
            linear(1)
            for i in range(HT):
                if i + 2 < HT:
                    linear(i + 2)
                act.wait_ge(s_z, i + 1)
                nc.scalar.activation(big[:, i % W], big[:, i % W], ACT.Exp).then_inc(s_e, 1)

        @block.tensor
        def _(pe):
            pe.wait_ge(s_junk, HT)
            nc.tensor.transpose(acc[0:HT, 0, 0:P], sc[:, 0].rearrange("p h t -> p (h t)"), ident[:]).then_inc(s_tr, 1)
            if make_neg:
                for t in range(T):
                    if t:
                        pe.wait_ge(s_neg, t)
                    for s in range(T):
                        last = nc.tensor.transpose(tp[:, s * P:(s + 1) * P], C0[:, s, t * P:(t + 1) * P], ident[:])
                    last.then_inc(s_ct, 1)
            if make_neg:
                pe.wait_ge(s_neg, T)
            for h in range(H):
                pe.wait_ge(s_uv, h + 1)
                if h >= 2:
                    pe.wait_ge(s_row, h)
                nc.tensor.transpose(tp[0:2 * T, 512 * (h % 2):512 * (h % 2) + P],
                                    uv[:, h].rearrange("p w t -> p (w t)"), ident[:]).then_inc(s_tr, 1)
            pe.wait_ge(s_row, 1)
            for h in range(H):
                for k in range(T):
                    pe.wait_ge(s_w, h * T + k + 1)
                    for t in range(T):
                        if h and k == 0 and t % 2 == 0:
                            pe.wait_ge(s_o, T * (h - 1) + t + 2)
                        last = nc.tensor.matmul(acc[:, t, 0:C + 1], big[:, k % W, t * P:(t + 1) * P], he[:, k, h, :],
                                                start=(k == 0 and t % 2 == 0), stop=(k == T - 1),
                                                skip_group_check=True)
                    last.then_inc(s_used, 1)


def project2(nc, A, ctx, sb, pb, sem, ident, out1, h2e, dims):
    T, D, DK, H2, C2 = (dims[k] for k in ("T", "D", "DK", "H2", "C2"))
    w2 = sb(ctx, "w2", [P, DK, H2 * C2], F32)
    oT = [sb(ctx, f"oT{i}", [P, DK, P], F32) for i in range(2)]
    tp = [pb(ctx, f"o_turn{i}", [P, 1024]) for i in range(2)]
    hp = [pb(ctx, f"h2_ps{i}", [P, 512]) for i in range(2)]
    s_w, s_one, s_tr, s_oT, s_mm, s_h2 = (sem(ctx, x) for x in (
        "w2_in", "ones_set", "o_turned", "oT_copied", "h2_done", "h2_copied"))
    with nc.Block() as block:
        @block.sync
        def _(sp):
            sp.dma_start(w2[:], A["L0_gnn_W2"].rearrange("(k p) n -> p k n", p=P)).then_inc(s_w, 16)

        @block.gpsimd
        def _(pool):
            pool.memset(h2e[:, :, :, C2:C2 + 1], 1.0).then_inc(s_one, 1)

        @block.tensor
        def _(pe):
            pe.wait_ge(s_w, 16)

            def turn(t):
                if t >= 2:
                    pe.wait_ge(s_oT, t - 1)
                for k in range(DK):
                    last = nc.tensor.transpose(tp[t % 2][:, k * P:(k + 1) * P], out1[:, t, k * P:(k + 1) * P], ident[:])
                last.then_inc(s_tr, 1)

            turn(0)
            for t in range(T):
                if t + 1 < T:
                    turn(t + 1)
                pe.wait_ge(s_oT, t + 1)
                if t >= 2:
                    pe.wait_ge(s_h2, t - 1)
                for k in range(DK):
                    last = nc.tensor.matmul(hp[t % 2][:, 0:H2 * C2], oT[t % 2][:, k, :], w2[:, k, :],
                                            start=(k == 0), stop=(k == DK - 1))
                last.then_inc(s_mm, 1)

        @block.scalar
        def _(act):
            for t in range(T):
                act.wait_ge(s_tr, t + 1)
                if t >= 2:
                    act.wait_ge(s_mm, t - 1)
                nc.scalar.copy(oT[t % 2][:].rearrange("p k n -> p (k n)"), tp[t % 2][:, 0:D]).then_inc(s_oT, 1)

        @block.vector
        def _(dve):
            for t in range(T):
                dve.wait_ge(s_mm, t + 1)
                nc.vector.tensor_copy(h2e[:, t, :, 0:C2],
                                      hp[t % 2][:, 0:H2 * C2].rearrange("p (h c) -> p h c", h=H2)).then_inc(s_h2, 1)


def update_x(nc, A, ctx, sb, pb, sem, ident, out2, x2_dram, dims):
    T, D, HC = dims["T"], dims["D"], dims["H2"] * dims["C2"]
    HALF = D // 2
    K1 = HC - P
    wa = sb(ctx, "wu_a", [P, D], F32)
    wb = sb(ctx, "wu_b", [K1, D], F32)
    oa = [sb(ctx, f"out2T_a{i}", [P, P], F32) for i in range(2)]
    ob = [sb(ctx, f"out2T_b{i}", [K1, P], F32) for i in range(2)]
    part = [sb(ctx, f"x2_part{i}", [P, D], F32) for i in range(2)]
    tp = [pb(ctx, f"out2_turn{i}", [P, 256]) for i in range(2)]
    y = [pb(ctx, f"x2_ps{i}", [P, 1024]) for i in range(2)]
    s_w, s_tr, s_oT, s_mm, s_x2 = (sem(ctx, x) for x in ("wu2_in", "out2_turned", "out2T_copied", "y2_done", "x2_summed"))
    s_in = [sem(ctx, f"x2_part_in{i}") for i in range(2)]
    s_st = [sem(ctx, f"x2_final_stored{i}") for i in range(2)]
    with nc.Block() as block:
        @block.sync
        def _(sp):
            sp.dma_start(wa[:], A["L0_gnn_Wu"][D:D + P]).then_inc(s_w, 16)
            sp.dma_start(wb[:], A["L0_gnn_Wu"][D + P:D + HC]).then_inc(s_w, 16)

            def load(t):
                if t >= 2:
                    sp.wait_ge(s_st[t % 2], 16 * (t // 2))
                sp.dma_start(part[t % 2][:], x2_dram[t * P:(t + 1) * P]).then_inc(s_in[t % 2], 16)

            load(0)
            load(1)
            for t in range(T):
                sp.wait_ge(s_x2, t + 1)
                sp.dma_start(x2_dram[t * P:(t + 1) * P], part[t % 2][:]).then_inc(s_st[t % 2], 16)
                if t + 2 < T:
                    load(t + 2)
            for i in range(2):
                sp.wait_ge(s_st[i], 16 * (T // 2))

        @block.tensor
        def _(pe):
            pe.wait_ge(s_w, 32)

            def turn(t):
                if t >= 2:
                    pe.wait_ge(s_oT, t - 1)
                nc.tensor.transpose(tp[t % 2][:, 0:P], out2[:, t, 0:P], ident[:])
                nc.tensor.transpose(tp[t % 2][0:K1, P:2 * P], out2[:, t, P:HC], ident[:]).then_inc(s_tr, 1)

            turn(0)
            for t in range(T):
                if t + 1 < T:
                    turn(t + 1)
                pe.wait_ge(s_oT, t + 1)
                if t >= 2:
                    pe.wait_ge(s_x2, t - 1)
                for c in range(2):
                    dst = y[t % 2][:, 512 * c:512 * c + HALF]
                    nc.tensor.matmul(dst, oa[t % 2][:], wa[:, c * HALF:(c + 1) * HALF], start=True, stop=False)
                    last = nc.tensor.matmul(dst, ob[t % 2][:], wb[:, c * HALF:(c + 1) * HALF], start=False, stop=True)
                last.then_inc(s_mm, 1)

        @block.scalar
        def _(act):
            for t in range(T):
                act.wait_ge(s_tr, t + 1)
                if t >= 2:
                    act.wait_ge(s_mm, t - 1)
                nc.scalar.copy(oa[t % 2][:], tp[t % 2][:, 0:P])
                nc.scalar.copy(ob[t % 2][:], tp[t % 2][0:K1, P:2 * P]).then_inc(s_oT, 1)

        @block.vector
        def _(dve):
            for t in range(T):
                dve.wait_ge(s_mm, t + 1)
                dve.wait_ge(s_in[t % 2], 16 * (t // 2 + 1))
                p = part[t % 2][:].rearrange("p (c n) -> p c n", c=2)
                nc.vector.tensor_tensor(p, p, y[t % 2][:].rearrange("p (c n) -> p c n", c=2)[:, :, 0:HALF],
                                        ALU.add).then_inc(s_x2, 1)


def rgcn(nc, A, ctx, sb, pb, sem, ident, inv, x2_dram, counts_dram, out, dims):
    T, NP, N, D, DK, LAST, R = (dims[k] for k in ("T", "NP", "N", "D", "DK", "LAST", "R"))
    TD, D1 = dims["TD"], dims["D1"]
    KT = [D1 // P, D1 // P, DK]
    NO = [D1, D, D]
    NC = [n // 2 for n in NO]
    L = len(KT)
    KM, NM = max(KT), max(NC)
    TASKS, AGGS = 2 * (R + 1), 2 * R
    CS, BANKS = 5, 4
    piece0 = [TASKS * sum(KT[:i]) for i in range(L)]
    assert D1 == D + TD and TD == P and (2 * T) % BANKS == 0 and T % CS == 0

    hTh = sb(ctx, "hT_hi", [P, KM, NP], F32R)
    hTl = sb(ctx, "hT_lo", [P, KM, NP], F32R)
    acc = sb(ctx, "acc", [P, T, max(NO)], F32)
    xwh = sb(ctx, "xw_hi", [P, T, NM], F32R)
    xwl = sb(ctx, "xw_lo", [P, T, NM], F32R)
    wh = sb(ctx, "w_hi", [P, KM, NM], F32R)
    wl = sb(ctx, "w_lo", [P, KM, NM], F32R)
    raw = sb(ctx, "w_raw", [P, 2, NM], F32)
    cnt = sb(ctx, "count_slots", [P, CS, T * P], F32R)
    bias = sb(ctx, "bias_bc", [P, max(NO)], F32)
    emb = sb(ctx, "emb", [R, TD], F32)
    eps = sb(ctx, "eps3", [P, 1], F32)
    part_id = sb(ctx, "part_id", [R, 1], F32)
    st = sb(ctx, "bn3", [P, T, 2, 6], F32)
    mv = sb(ctx, "mean_var3", [P, 5, T], F32)
    tps = pb(ctx, "xw_ps", [P, BANKS, 512])
    aps = pb(ctx, "agg_ps", [P, 2, 1024])

    def agg_bank(i):
        return aps[:, (i % BANKS) // 2, 512 * (i % 2):512 * (i % 2) + 512]

    names = ("eps3_set", "emb_in", "mean_step", "affine3", "sd3", "h3_ready", "onehot_ready", "turned3", "hT_ready",
             "hT_hi_ready", "w_hi_ready", "w_lo_ready", "xw_done", "xw_free", "xw_hi_ready", "agg_done", "agg_free", "bias_set", "final")
    (s_set, s_emb, s_bn, s_aff, s_sd, s_h, s_hot, s_turn, s_hT, s_hTh, s_wh, s_wl, s_tps, s_tfree, s_xwh,
     s_aps, s_afree, s_bi, s_fin) = (sem(ctx, x) for x in names)
    s_x2 = [sem(ctx, f"x2_in{t}") for t in range(2)]
    s_raw = [sem(ctx, f"w_raw_in{i}") for i in range(2)]
    s_cnt = [sem(ctx, f"counts_in{i}") for i in range(CS)]
    s_bias, s_granted = sem(ctx, "bias_in"), sem(ctx, "count_slot_granted")
    s_res = [sem(ctx, f"x2_again{i}") for i in range(CS)]
    s_out = sem(ctx, "out_stored")
    walls = [A[f"w_all{i + 1}"] for i in range(L)]

    def piece(l, q, k):
        return piece0[l] + KT[l] * q + k

    def slot(l, parity, k):
        return (KT[l] * parity + k) % 2

    def raw_count(l, pair, parity, k):
        i = slot(l, parity, k)
        before = TASKS // 2 * sum(KT[:l])
        own = len([j for j in range(k + 1) if slot(l, parity, j) == i])
        if parity:
            own += len([j for j in range(KT[l]) if slot(l, 0, j) == i])
        return 16 * (before + own) + 16 * KT[l] * pair

    with nc.Block() as block:
        @block.sync
        def _(sp):
            for i, (a, b) in enumerate(((0, 2), (2, T))):
                sp.dma_start(acc[:, a:b, 0:D],
                             x2_dram[a * P:b * P].rearrange("(t p) d -> p t d", p=P)).then_inc(s_x2[i], 16)
            sp.dma_start(emb[:], A["L1_gnn_node_emb"]).then_inc(s_emb, 16)
            sp.wait_ge(s_set, 1)
            kinds = A["node_type_3"]
            full = (T - 1) * P
            types = acc[0:R, :, D:D + P].bitcast(I32)
            sp.dma_start(types[:, 0:T - 1, :], kinds[0:full].rearrange("(a t p) -> a t p", a=1, p=P)
                         .to_broadcast([R, T - 1, P])).then_inc(s_emb, 16)
            sp.dma_start(types[:, T - 1, 0:LAST], kinds[full:N].rearrange("(a p) -> a p", a=1)
                         .to_broadcast([R, LAST])).then_inc(s_emb, 16)

            def weights(l, q, matrix, c, parity):
                for k in range(KT[l]):
                    i = slot(l, parity, k)
                    p = piece(l, q, k)
                    if not (isinstance(p, int) and p < 2):
                        sp.wait_ge(s_wl, p - 1)
                    src = walls[l][matrix] if isinstance(matrix, int) else \
                        walls[l][ds(matrix, 1)].rearrange("o k n -> (o k) n")
                    sp.dma_start(raw[:, i, 0:NC[l]],
                                 src[k * P:(k + 1) * P, c * NC[l]:(c + 1) * NC[l]]).then_inc(s_raw[i], 16)

            for l in range(L):
                weights(l, 0, 0, 0, 0)
                with sp.Fori(0, R) as r:
                    weights(l, 2 * r + 1, r, 1, 1)
                    weights(l, 2 * r + 2, r + 1, 0, 0)
                weights(l, 2 * R + 1, R, 1, 1)
            for t in range(T):
                sp.wait_ge(s_aps, L * AGGS * T + CS)
                if t >= CS:
                    sp.wait_ge(s_fin, t - CS + 1)
                sp.dma_start(cnt[:, t % CS, 0:D].bitcast(F32), x2_dram[t * P:(t + 1) * P]).then_inc(s_res[t % CS], 16)
            for t in range(T):
                sp.wait_ge(s_fin, t + 1)
                n = P if t < T - 1 else LAST
                sp.dma_start(out[t * P:t * P + n], acc[0:n, t, 0:D]).then_inc(s_out, 16)
            sp.wait_ge(s_out, 16 * T)

        @block.gpsimd
        def _(pool):
            pool.memset(acc[0:R, T - 1, D:D + P].bitcast(I32), 0).then_inc(s_set, 1)
            pool.memset(eps[:], EPS).then_inc(s_set, 1)
            pool.iota(part_id[:], [[1, 1]], base=0, channel_multiplier=1,
                      allow_small_or_imprecise_dtypes=True).then_inc(s_set, 1)
            for l in range(L):
                if l:
                    pool.wait_ge(s_bi, l)
                pool.dma_start(bias[:, 0:NO[l]], A[f"L1_gnn_b{l + 1}"].rearrange("(a d) -> a d", a=1)
                               .to_broadcast([P, NO[l]])).then_inc(s_bias, 16)
                with pool.Fori(0, R) as r:
                    for c in range(2):
                        for t in range(T):
                            g = AGGS * l + 2 * r + c
                            pool.wait_ge(s_aps, T * g + t + 1)
                            pool.sem_inc(s_granted, 1)
                            pool.dma_start(cnt[:, t % CS, :].bitcast(F32),
                                           counts_dram[ds(r, 1), t].rearrange("o p n -> (o p) n")
                                           ).then_inc(s_cnt[t % CS], 16)

        @block.tensor
        def _(pe):
            pe.sem_inc(s_aps, CS)
            pe.wait_ge(s_emb, 48)

            def turn(l):
                kt = KT[l]
                for t in range(T):
                    if l == 0:
                        pe.wait_ge(s_h, t + 1)
                        pe.wait_ge(s_hot, 1)
                    else:
                        pe.wait_ge(s_tfree, T * (TASKS * l - 1) + t + 1 + BANKS)
                        if t < 2:
                            pe.wait_ge(s_afree, AGGS * T * l + BANKS)
                    if t >= 2:
                        pe.wait_ge(s_hT, T * l + t - 1)
                    for k in range(DK if l == 0 else kt):
                        last = nc.tensor.transpose(aps[:, t % 2, k * P:(k + 1) * P], acc[:, t, k * P:(k + 1) * P],
                                                   ident[:])
                    if l == 0:
                        last = nc.tensor.matmul(aps[:, t % 2, D:D + TD], emb[:], acc[0:R, t, D:D + P],
                                                start=True, stop=True, skip_group_check=True)
                    last.then_inc(s_turn, 1)

            def transform(l, q, parity):
                task = TASKS * l + q
                for m in range(T):
                    bank = tps[:, (T * parity + m) % BANKS, 0:NC[l]]
                    pe.wait_ge(s_tfree, T * task + m + 1)
                    for k in range(KT[l]):
                        if m == 0:
                            pe.wait_ge(s_wl, piece(l, q, k) + 1)
                        hi, lo = hTh[:, k, m * P:(m + 1) * P], hTl[:, k, m * P:(m + 1) * P]
                        nc.tensor.matmul(bank, hi, wh[:, k, 0:NC[l]], start=(k == 0), stop=False)
                        nc.tensor.matmul(bank, hi, wl[:, k, 0:NC[l]], start=False, stop=False)
                        last = nc.tensor.matmul(bank, lo, wh[:, k, 0:NC[l]], start=False, stop=(k == KT[l] - 1))
                    last.then_inc(s_tps, 1)

            def aggregate(l, r, c):
                g = AGGS * l + 2 * r + c
                for t in range(T):
                    bank = agg_bank(T * c + t)[:, 0:NC[l]]
                    pe.wait_ge(s_afree, T * g + t + 1)
                    pe.wait_ge(s_cnt[t % CS], 16 * ((T // CS) * g + t // CS + 1))
                    for s in range(T):
                        if t == 0:
                            pe.wait_ge(s_tfree, T * (TASKS * l + 2 * r + c) + s + 1 + BANKS)
                        lhs = cnt[:, t % CS, s * P:(s + 1) * P]
                        nc.tensor.matmul(bank, lhs, xwh[:, s, 0:NC[l]], start=(s == 0), stop=False)
                        last = nc.tensor.matmul(bank, lhs, xwl[:, s, 0:NC[l]], start=False, stop=(s == T - 1))
                    last.then_inc(s_aps, 1)

            for l in range(L):
                turn(l)
                pe.wait_ge(s_hT, T * (l + 1))
                with pe.Fori(0, R) as r:
                    for c in range(2):
                        transform(l, 2 * r + c, c)
                        aggregate(l, r, c)
                for c in range(2):
                    transform(l, 2 * R + c, c)

        @block.scalar
        def _(act):
            act.wait_ge(s_set, 3)
            act.wait_ge(s_bn, 2)
            nc.scalar.activation(mv[:, 2, :], mv[:, 1, :], ACT.Sqrt, bias=eps[:]).then_inc(s_sd, 1)
            act.wait_ge(s_aff, 1)
            for t in range(T):
                nc.scalar.activation(acc[:, t, 0:D], acc[:, t, 0:D], ACT.Relu, bias=mv[:, 4, t:t + 1],
                                     scale=mv[:, 3, t:t + 1]).then_inc(s_h, 1)

            def split(l, pair, parity):
                task = TASKS * l + 2 * pair + parity
                for k in range(KT[l]):
                    i = slot(l, parity, k)
                    if k == 0 and not (isinstance(task, int) and task == 0):
                        act.wait_ge(s_tps, T * task)
                    act.wait_ge(s_raw[i], raw_count(l, pair, parity, k))
                    nc.scalar.copy(wh[:, k, 0:NC[l]], raw[:, i, 0:NC[l]]).then_inc(s_wh, 1)

            def turned(l):
                kt = KT[l]
                for t in range(T):
                    act.wait_ge(s_turn, T * l + t + 1)
                    nc.scalar.activation(hTh[:, 0:kt, t * P:(t + 1) * P],
                                         aps[:, t % 2, 0:kt * P].rearrange("p (k n) -> p k n", k=kt),
                                         ACT.Copy if l == 0 else ACT.Relu).then_inc(s_hTh, 1)

            def hi_part(l, r, c):
                g = AGGS * l + 2 * r + c
                for m in range(T):
                    act.wait_ge(s_tps, T * (TASKS * l + 2 * r + c) + m + 1)
                    if m == 0:
                        act.wait_ge(s_aps, T * g + CS)
                    nc.scalar.copy(xwh[:, m, 0:NC[l]], tps[:, (T * c + m) % BANKS, 0:NC[l]]).then_inc(s_xwh, 1)

            for l in range(L):
                split(l, 0, 0)
                turned(l)
                with act.Fori(0, R) as r:
                    hi_part(l, r, 0)
                    split(l, r, 1)
                    hi_part(l, r, 1)
                    split(l, r + 1, 0)
                split(l, R, 1)

        @block.vector
        def _(dve):
            dve.sem_inc(s_tfree, BANKS)
            dve.sem_inc(s_afree, BANKS)
            for i, (a, b) in enumerate(((0, 2), (2, T))):
                dve.wait_ge(s_x2[i], 16)
                for t in range(a, b):
                    for c in range(2):
                        last = nc.vector.bn_stats(st[:, t, c, :], acc[:, t, c * (D // 2):(c + 1) * (D // 2)])
            last.then_inc(s_bn, 1)
            dve.wait_ge(s_bn, 1)
            for t in range(T):
                last = nc.vector.bn_aggr(mv[:, 0:2, t], st[:, t].rearrange("p c s -> p (c s)"))
            last.then_inc(s_bn, 1)
            dve.wait_ge(s_sd, 1)
            nc.vector.reciprocal(mv[:, 3, :], mv[:, 2, :]).then_inc(s_bn, 1)
            dve.wait_ge(s_bn, 3)
            nc.vector.scalar_tensor_tensor(mv[:, 4, :], mv[:, 0, :], -1.0, mv[:, 3, :], ALU.mult,
                                           ALU.mult).then_inc(s_aff, 1)
            dve.wait_ge(s_emb, 48)
            dve.wait_ge(s_set, 3)
            hot = acc[0:R, :, D:D + P]
            nc.vector.tensor_scalar(hot, hot.bitcast(I32), part_id[:], None, ALU.is_equal).then_inc(s_hot, 1)

            def split_piece(l, q, parity, k):
                dve.wait_ge(s_wh, piece(l, q, k) + 1)
                nc.vector.tensor_tensor(wl[:, k, 0:NC[l]], raw[:, slot(l, parity, k), 0:NC[l]],
                                        wh[:, k, 0:NC[l]].bitcast(F32), ALU.subtract).then_inc(s_wl, 1)

            def turned(l):
                kt = KT[l]
                for t in range(T):
                    dve.wait_ge(s_hTh, T * l + t + 1)
                    hi = hTh[:, 0:kt, t * P:(t + 1) * P].bitcast(F32)
                    lo = hTl[:, 0:kt, t * P:(t + 1) * P]
                    ps = aps[:, t % 2, 0:kt * P].rearrange("p (k n) -> p k n", k=kt)
                    if l == 0:
                        nc.vector.tensor_tensor(lo, ps, hi, ALU.subtract).then_inc(s_hT, 1)
                    else:
                        nc.vector.scalar_tensor_tensor(lo, ps, 0.0, hi, ALU.max, ALU.subtract).then_inc(s_hT, 1)

            def lo_part(l, r, c):
                for m in range(T):
                    g = AGGS * l + 2 * r + c
                    dve.wait_ge(s_xwh, T * g + m + 1)
                    nc.vector.tensor_tensor(xwl[:, m, 0:NC[l]], tps[:, (T * c + m) % BANKS, 0:NC[l]],
                                            xwh[:, m, 0:NC[l]].bitcast(F32), ALU.subtract).then_inc(s_tfree, 1)

            def add_means(l, r, c, nxt):
                for t in range(T):
                    if t < KT[l]:
                        split_piece(l, *nxt, t)
                    g = AGGS * l + 2 * r + c
                    dve.wait_ge(s_aps, T * g + t + 1 + CS)
                    a = acc[:, t, c * NC[l]:(c + 1) * NC[l]]
                    nc.vector.scalar_tensor_tensor(a, agg_bank(T * c + t)[:, 0:NC[l]], inv[:, t, ds(r, 1)], a,
                                                   ALU.mult, ALU.add).then_inc(s_afree, 1)

            for l in range(L):
                for k in range(KT[l]):
                    split_piece(l, 0, 0, k)
                turned(l)
                dve.wait_ge(s_bias, 16 * (l + 1))
                dve.wait_ge(s_turn, T * (l + 1))
                for t in range(T):
                    last = nc.vector.tensor_copy(acc[:, t, 0:NO[l]], bias[:, 0:NO[l]])
                last.then_inc(s_bi, 1)
                dve.wait_ge(s_bi, l + 1)
                with dve.Fori(0, R) as r:
                    for c in range(2):
                        lo_part(l, r, c)
                        add_means(l, r, c, (2 * r + c + 1, 1 - c))
                for c in range(2):
                    for t in range(T):
                        dve.wait_ge(s_tps, T * (TASKS * l + 2 * R + c) + t + 1)
                        if c == 0 and t == 0:
                            dve.wait_ge(s_afree, T * AGGS * (l + 1) + BANKS)
                        a = acc[:, t, c * NC[l]:(c + 1) * NC[l]]
                        nc.vector.tensor_tensor(a, tps[:, (T * c + t) % BANKS, 0:NC[l]], a, ALU.add).then_inc(s_tfree, 1)
                    if c == 0:
                        for k in range(KT[l]):
                            split_piece(l, 2 * R + 1, 1, k)
            dve.wait_ge(s_tfree, T * TASKS * L + BANKS)
            for t in range(T):
                dve.wait_ge(s_res[t % CS], 16 * (t // CS + 1))
                nc.vector.scalar_tensor_tensor(acc[:, t, 0:D], acc[:, t, 0:D], 0.0, cnt[:, t % CS, 0:D].bitcast(F32),
                                               ALU.max, ALU.add).then_inc(s_fin, 1)


_OUT = ((1250, 768), "float32")


def kernel(**inputs):
    import numpy as np
    import concourse.bacc as bacc
    from concourse.bass_utils import run_bass_kernel_spmd

    nc = bacc.Bacc("TRN2", target_bir_lowering=False, num_devices=1)
    arrays, aps = {}, {}
    for i in (1, 2, 3):
        inputs[f"w_all{i}"] = np.concatenate([np.asarray(inputs.pop(f"L1_gnn_w_rel{i}")),
                                              np.asarray(inputs.pop(f"L1_gnn_w_root{i}"))[None]])
    for name, value in inputs.items():
        a = np.ascontiguousarray(value)
        arrays[f"in_{name}"] = a
        aps[name] = nc.dram_tensor(f"in_{name}", a.shape, mybir.dt.from_np(a.dtype), kind="ExternalInput").ap()
    out = nc.dram_tensor("out", _OUT[0], F32, kind="ExternalOutput").ap()
    gnn_kernel(nc, aps, out)
    r = run_bass_kernel_spmd(nc, [arrays], core_ids=[0])
    return r.results[0]["out"]
```

```python
from contextlib import ExitStack

import concourse.bass as bass
from concourse import mybir

ALU = mybir.AluOpType
ACT = mybir.ActivationFunctionType
AX = mybir.AxisListType
F32 = mybir.dt.float32
F32R = mybir.dt.float32r
BF16 = mybir.dt.bfloat16
I16 = mybir.dt.int16
I32 = mybir.dt.int32

P = 128
EPS = 1e-5
SLOPE = 0.2
NEG = -1e30
TYPE_STEP = 4096
GROUP = 32


def ds(start, size):
    return bass.ds(start, size)


def gnn_kernel(nc, A, out):
    N, D = A["x"].shape
    E = A["src"].shape[0]
    R, D1 = A["w_all1"].shape[0] - 1, A["w_all1"].shape[1]
    TD = A["L1_gnn_node_emb"].shape[1]
    H1, C1 = A["L0_gnn_a_src1"].shape
    H2, C2 = A["L0_gnn_a_src2"].shape
    T = -(-N // P)
    NP = T * P
    LAST = N - (T - 1) * P
    DK = D // P
    ET = -(-E // P)
    EA, EB = P * P, ET - P
    EFULL = E // P - P
    NG = NP // GROUP
    GC = R * GROUP
    QG = P // GROUP
    SB = 512 // GC
    ETP = -(-ET // 2)
    assert SB * 2 >= T and D % P == 0 and T % 2 == 0 and EFULL >= 0

    root = ExitStack()

    def sb(ctx, name, shape, dt):
        return ctx.enter_context(nc.sbuf_tensor(name, shape, dt))

    def pb(ctx, name, shape, dt=F32):
        return ctx.enter_context(nc.psum_tensor(name, shape, dt))

    def sem(ctx, name):
        return ctx.enter_context(nc.semaphore(name))

    counts_dram = nc.dram_tensor("counts_scratch", [R, T, P, T * P], F32, kind="Internal").ap()
    x2_dram = nc.dram_tensor("x2_scratch", [NP, D], F32, kind="Internal").ap()
    arow_dram = [nc.dram_tensor(f"arow_scratch{i}", [H * T, P], F32, kind="Internal").ap()
                 for i, H in enumerate((H1, H2))]
    uvrow_dram = [nc.dram_tensor(f"uvrow_scratch{i}", [2 * H * T, P], F32, kind="Internal").ap()
                  for i, H in enumerate((H1, H2))]

    with root:
        ident = sb(root, "ident", [P, P], F32)
        inv = sb(root, "inv", [P, R, T], F32)
        inv_g = sb(root, "inv_by_group", [GC, QG, T], F32)
        gat = ExitStack()
        with gat:
            C0 = sb(gat, "C0", [P, T, NP], F32)
            h1e = sb(gat, "h1e", [P, T, H1, C1 + 1], F32)
            with ExitStack() as first:
                x = sb(first, "x", [P, T, D], F32)
                w1 = sb(first, "w1", [P, DK, D], F32)
                wu = sb(first, "wu", [P, DK, D], F32)
                gb = sb(first, "norm_gb", [P, 2, DK], F32)
                bu = sb(first, "bu", [P, D], F32)
                s_xpad, s_x, s_w, s_gb = (sem(first, n) for n in ("x_padded", "x_in", "w_in", "gb_in"))
                with ExitStack() as ctx:
                    count_edges(nc, A, ctx, sb, pb, sem, ident, inv_g, C0, counts_dram, locals())
                with ExitStack() as ctx:
                    norm_and_project(nc, A, ctx, sb, pb, sem, ident, inv_g, inv, h1e, x2_dram, locals())
            neg = sb(gat, "neg", [P, T, NP], BF16)
            out1 = sb(gat, "out1", [P, T, D], F32)
            with ExitStack() as ctx:
                gat_attention(nc, A, ctx, sb, pb, sem, ident, C0, neg, h1e, out1, H1, C1, "1",
                              arow_dram[0], uvrow_dram[0], True, locals())
            h2e = sb(gat, "h2e", [P, T, H2, C2 + 1], F32)
            with ExitStack() as ctx:
                project2(nc, A, ctx, sb, pb, sem, ident, out1, h2e, locals())
            out2 = out1[:, :, 0:H2 * C2]
            with ExitStack() as ctx:
                gat_attention(nc, A, ctx, sb, pb, sem, ident, C0, neg, h2e, out2, H2, C2, "2",
                              arow_dram[1], uvrow_dram[1], False, locals())
            with ExitStack() as ctx:
                update_x(nc, A, ctx, sb, pb, sem, ident, out2, x2_dram, locals())
        with ExitStack() as ctx:
            rgcn(nc, A, ctx, sb, pb, sem, ident, inv, x2_dram, counts_dram, out, locals())


def count_edges(nc, A, ctx, sb, pb, sem, ident, inv_g, C0, counts_dram, dims):
    T, NP, ET, EA, EB, EFULL = (dims[k] for k in ("T", "NP", "ET", "EA", "EB", "EFULL"))
    NG, GC, QG, SB, ETP, R, E = (dims[k] for k in ("NG", "GC", "QG", "SB", "ETP", "R", "E"))
    PAIR = 2 * QG

    raw = sb(ctx, "edges_raw", [P, 3, 2, P], I32)
    edges = sb(ctx, "edges_f", [P, 3, 2, P], F32)
    key = edges[:, 2]
    src_col = sb(ctx, "src_col", [P, 2 * P], F32)
    key_col = sb(ctx, "key_col", [P, 2 * P], F32)
    iota_src = sb(ctx, "iota_src", [P, NP], I16)
    iota_key = sb(ctx, "iota_key", [P, NG * GC], I16)
    ones = sb(ctx, "count_ones", [P, P], F32)
    ones_b = sb(ctx, "count_ones_b", [P, 1], BF16)
    span = sb(ctx, "tile_span", [P, 2, 2], F32)
    span_b = sb(ctx, "tile_span_b", [P, 2, 2, NG], F32)
    jcol = sb(ctx, "jcol", [NG, ETP], F32)
    gcol = sb(ctx, "gcol", [NG, 2], F32)
    tri = sb(ctx, "tri", [NG, NG], F32)
    pair_span = sb(ctx, "pair_span", [NG, 2, ETP], F32)
    hit = edges[0:NG, 0:2].rearrange("g a h p -> g (a h p)")[:, 0:3 * ETP].rearrange("g (m j) -> g m j", m=3)
    rng = sb(ctx, "rng", [NG, 6], F32)
    spans_i = sb(ctx, "spans_i", [1, 2 * NG], I32)
    shifted = sb(ctx, "shifted", [1, NG], I32)
    table = sb(ctx, "table", [1, NG], I32)
    SPAN_BITS = ((ETP - 1) * P + ETP).bit_length()
    hot_src = sb(ctx, "hot_src", [P, 2, NP], BF16)
    hot_key = sb(ctx, "hot_key", [P, 2, GC], BF16)
    stage = [sb(ctx, f"count_stage{i}", [P, R, T, P], F32R) for i in range(2)]
    zero_b = sb(ctx, "zero_b", [P, 512], BF16)

    cnt_ps = [[pb(ctx, f"cnt_ps{i}{b}", [P, 512]) for b in range(2)] for i in range(2)]
    misc = pb(ctx, "misc_ps", [P, 512])
    deg = pb(ctx, "deg_ps", [P, 512])

    s_pad, s_load, s_edge_f, s_const = (sem(ctx, n) for n in ("pad_set", "edges_in", "edges_conv", "consts"))
    s_tr, s_cols, s_dve, s_bc, s_pre, s_row, s_table = (sem(ctx, n) for n in (
        "edges_turned", "cols_ready", "dve_step", "span_bc", "visits_summed", "row_ready", "table_ready"))
    s_free, s_hot, s_group, s_copied = (sem(ctx, n) for n in ("slot_free", "hot_ready", "group_done", "group_copied"))
    s_inv, s_c0 = (sem(ctx, n) for n in ("inv_done", "c0_tile_done"))
    s_out = [sem(ctx, f"counts_stored{i}") for i in range(2)]
    s_spanb = sem(ctx, "span_copied")

    def ranges(eng):
        def read(g):
            word = eng.value_load(table[0:1, ds(g, 1)], min_val=0, max_val=((NG + 1) * ETP << SPAN_BITS) - 1)
            return word % (1 << SPAN_BITS) // P, word % P, word // (1 << SPAN_BITS)
        return read

    with nc.Block() as block:
        @block.sync
        def _(sp):
            sp.wait_ge(s_pad, 1)
            for i, name in enumerate(("src", "dst", "edge_type_3")):
                a = A[name]
                sp.dma_start(raw[:, i, 0, :], a[0:EA].rearrange("(j p) -> j p", p=P)).then_inc(s_load, 16)
                if EFULL:
                    sp.dma_start(raw[0:EFULL, i, 1, :],
                                 a[EA:EA + EFULL * P].rearrange("(j p) -> j p", p=P)).then_inc(s_load, 16)
                if EB > EFULL:
                    rest = E - EA - EFULL * P
                    sp.dma_start(raw[EFULL:EB, i, 1, 0:rest],
                                 a[EA + EFULL * P:E].rearrange("(j p) -> j p", j=1)).then_inc(s_load, 16)
            x, w1, wu, gb, bu = (dims[k] for k in ("x", "w1", "wu", "gb", "bu"))
            s_xpad, s_x, s_w, s_gb, D, LAST = (dims[k] for k in ("s_xpad", "s_x", "s_w", "s_gb", "D", "LAST"))
            sp.wait_ge(s_xpad, 1)
            sp.dma_start(x[:, 0:T - 1, :], A["x"][0:(T - 1) * P].rearrange("(t p) d -> p t d", p=P)).then_inc(s_x, 16)
            sp.dma_start(x[0:LAST, T - 1, :], A["x"][(T - 1) * P:]).then_inc(s_x, 16)
            sp.dma_start(wu[:], A["L0_gnn_Wu"][0:D].rearrange("(k p) n -> p k n", p=P)).then_inc(s_w, 16)
            sp.dma_start(bu[:], A["L0_gnn_bu"].rearrange("(a d) -> a d", a=1).to_broadcast([P, D])).then_inc(s_w, 16)
            with nc.allow_non_contiguous_dma(reason="two vectors of one column per feature tile"):
                sp.dma_start(gb[:, 0, :], A["L0_gnn_norm_g"].rearrange("(k p) -> p k", p=P)).then_inc(s_gb, 16)
                sp.dma_start(gb[:, 1, :], A["L0_gnn_norm_b"].rearrange("(k p) -> p k", p=P)).then_inc(s_gb, 16)
            sp.dma_start(w1[:], A["L0_gnn_W1"].rearrange("(k p) n -> p k n", p=P)).then_inc(s_gb, 16)
            for half in range(2):
                sp.sem_inc(s_out[half], 16 * R)
            with sp.Fori(0, T // 2) as t2:
                for half in range(2):
                    sp.wait_ge(s_copied, PAIR * t2 + QG * (half + 1) + 2)
                    for r in range(R):
                        sp.dma_start(counts_dram[r, ds(2 * t2 + half, 1)].rearrange("o p n -> (o p) n"),
                                     stage[half][:, r].rearrange("p t d -> p (t d)").bitcast(F32)).then_inc(s_out[half], 16)
            for half in range(2):
                sp.wait_ge(s_out[half], 16 * R * (T // 2 + 1))

        @block.gpsimd
        def _(pool):
            pool.memset(dims["x"][:, T - 1, :], 0.0).then_inc(dims["s_xpad"], 1)
            pool.memset(ones[:], 1.0).then_inc(s_const, 1)
            pool.memset(zero_b[:], 0.0).then_inc(s_const, 1)
            pool.iota(iota_src[:], [[1, NP]], base=0, channel_multiplier=0,
                      allow_small_or_imprecise_dtypes=True).then_inc(s_const, 1)
            pool.iota(iota_key[:].rearrange("p (g r i) -> p g r i", g=NG, r=R),
                      [[GROUP, NG], [TYPE_STEP, R], [1, GROUP]], base=0, channel_multiplier=0,
                      allow_small_or_imprecise_dtypes=True).then_inc(s_const, 1)
            pool.iota(jcol[:], [[1, ETP]], base=0, channel_multiplier=0,
                      allow_small_or_imprecise_dtypes=True).then_inc(s_const, 1)
            pool.iota(gcol[:], [[GROUP - 1, 2]], base=0, channel_multiplier=GROUP,
                      allow_small_or_imprecise_dtypes=True).then_inc(s_const, 1)
            pool.wait_ge(s_const, 1)
            pool.affine_select(out=ident[:], in_=ones[:], compare_op=ALU.is_equal, fill=0.0, base=0,
                               pattern=[[-1, P]], channel_multiplier=1).then_inc(s_const, 1)
            pool.affine_select(out=tri[:], in_=ones[0:NG, 0:NG], compare_op=ALU.is_ge, fill=0.0, base=-1,
                               pattern=[[1, NG]], channel_multiplier=-1).then_inc(s_const, 1)
            pool.sem_inc(s_c0, 2)
            with pool.Fori(0, T // 2) as t2:
                for half in range(2):
                    t = 2 * t2 + half
                    pool.wait_ge(s_copied, PAIR * t2 + QG * (half + 1) + 2)
                    cols = C0[:, :, ds(t * P, P)]
                    st = stage[half]
                    pool.tensor_tensor(cols, st[:, 0].bitcast(F32), st[:, 1].bitcast(F32), ALU.add)
                    pool.drain()
                    pool.tensor_tensor(cols, cols, st[:, 2].bitcast(F32), ALU.add)
                    pool.drain()
                    diag = C0[:, ds(t, 1), ds(t * P, P)].rearrange("p o d -> p (o d)")
                    pool.tensor_tensor(diag, diag, ident[:], ALU.add).then_inc(s_c0, 1)

        N_CONST = 8

        @block.vector
        def _(dve):
            nc.vector.memset(raw[:, 0, 1, :], -1)
            nc.vector.memset(raw[:, 1, 1, :], NP - 1)
            nc.vector.memset(raw[:, 2, 1, :], R).then_inc(s_pad, 1)
            dve.wait_ge(s_load, 16 * 3 * (1 + (EFULL > 0) + (EB > EFULL)))
            step = 0
            nc.vector.tensor_copy(edges[:], raw[:]).then_inc(s_dve, 1)
            step += 1
            dve.wait_ge(s_dve, step)
            nc.vector.scalar_tensor_tensor(key, edges[:, 2], float(TYPE_STEP), edges[:, 1],
                                           ALU.mult, ALU.add).then_inc(s_edge_f, 1)
            nc.vector.tensor_reduce(span[:, :, 0:1], edges[:, 1], AX.X, ALU.min)
            nc.vector.tensor_reduce(span[:, :, 1:2], edges[:, 1], AX.X, ALU.max).then_inc(s_dve, 1)
            step += 1
            dve.wait_ge(s_dve, step)
            dve.wait_ge(s_const, N_CONST)
            for half in range(2):
                for m in range(2):
                    last = nc.vector.tensor_scalar(span_b[:, half, m, :], ones[:, 0:NG],
                                                   span[:, half, m:m + 1], None, ALU.mult)
            last.then_inc(s_spanb, 1)
            dve.wait_ge(s_tr, 1)
            nc.vector.tensor_copy(src_col[:], misc[:, 0:2 * P])
            nc.vector.tensor_copy(ones_b[:], ones[:, 0:1])
            nc.vector.tensor_copy(key_col[:], misc[:, 2 * P:4 * P]).then_inc(s_cols, 1)
            dve.wait_ge(s_bc, 1)
            for m, op in enumerate((ALU.min, ALU.max)):
                last = nc.vector.tensor_reduce(
                    pair_span[:, m, :], deg[0:NG, 256 * m:256 * m + 2 * ETP].rearrange("g (j two) -> g j two", two=2),
                    AX.X, op)
            last.then_inc(s_dve, 1)
            step += 1
            dve.wait_ge(s_dve, step)
            nc.vector.tensor_scalar(hit[:, 0], pair_span[:, 0], gcol[:, 1:2], None, ALU.is_le).then_inc(s_dve, 1)
            step += 1
            dve.wait_ge(s_dve, step)
            nc.vector.scalar_tensor_tensor(hit[:, 1], pair_span[:, 1], gcol[:, 0:1], hit[:, 0],
                                           ALU.is_ge, ALU.mult).then_inc(s_dve, 1)
            step += 1
            dve.wait_ge(s_dve, step)
            nc.vector.scalar_tensor_tensor(hit[:, 0], jcol[:], 1.0, hit[:, 1], ALU.add, ALU.mult)
            nc.vector.tensor_scalar(hit[:, 2], jcol[:], -1.0, float(2 * P), ALU.mult, ALU.add).then_inc(s_dve, 1)
            step += 1
            dve.wait_ge(s_dve, step)
            nc.vector.tensor_tensor(hit[:, 2], hit[:, 2], hit[:, 1], ALU.mult).then_inc(s_dve, 1)
            step += 1
            dve.wait_ge(s_dve, step)
            nc.vector.tensor_reduce(rng[:, 3:4], hit[:, 0], AX.X, ALU.max)
            nc.vector.tensor_reduce(rng[:, 4:5], hit[:, 2], AX.X, ALU.max).then_inc(s_dve, 1)
            step += 1
            dve.wait_ge(s_dve, step)
            nc.vector.tensor_scalar(rng[:, 1:2], rng[:, 3:4], 1.0, None, ALU.max).then_inc(s_dve, 1)
            nc.vector.tensor_scalar(rng[:, 5:6], rng[:, 4:5], -1.0, float(2 * P), ALU.mult, ALU.add).then_inc(s_dve, 1)
            step += 2
            dve.wait_ge(s_dve, step)
            nc.vector.scalar_tensor_tensor(rng[:, 0:1], rng[:, 1:2], -1.0, rng[:, 5:6],
                                           ALU.add, ALU.min).then_inc(s_dve, 1)
            step += 1
            dve.wait_ge(s_dve, step)
            nc.vector.tensor_tensor(rng[:, 3:4], rng[:, 1:2], rng[:, 0:1], ALU.subtract)
            nc.vector.tensor_scalar(rng[:, 4:5], rng[:, 0:1], -1.0, float(ETP), ALU.mult, ALU.add)
            nc.vector.scalar_tensor_tensor(rng[:, 2:3], rng[:, 0:1], float(P), rng[:, 1:2], ALU.mult,
                                           ALU.add).then_inc(s_row, 1)
            dve.wait_ge(s_pre, 1)
            nc.vector.tensor_copy(spans_i[:], misc[0:1, 0:2 * NG]).then_inc(s_dve, 1)
            step += 1
            dve.wait_ge(s_dve, step)
            nc.vector.tensor_scalar(shifted[:], spans_i[:, NG:2 * NG], SPAN_BITS, None,
                                    ALU.logical_shift_left).then_inc(s_table, 1)
            dve.wait_ge(s_table, 1)
            nc.vector.tensor_tensor(table[:], shifted[:], spans_i[:, 0:NG], ALU.bitwise_or).then_inc(s_table, 1)
            dve.wait_ge(s_table, 2)
            dve.sem_inc(s_hot, 2 * ETP)
            read = ranges(dve)
            with dve.Fori(0, NG) as g:
                lo, end, shift = read(g)
                with dve.Fori(lo, end) as j:
                    v = j + shift
                    for tile in range(2):
                        dve.wait_ge(s_free, 2 * v + tile + 1)
                        nc.vector.tensor_scalar(hot_src[:, tile], iota_src[:],
                                                src_col[:, ds(2 * j + tile, 1)], None, ALU.is_equal)
                        nc.vector.tensor_scalar(hot_key[:, tile], iota_key[:, ds(g * GC, GC)],
                                                key_col[:, ds(2 * j + tile, 1)], None,
                                                ALU.is_equal).then_inc(s_hot, 1)
            dve.wait_ge(s_group, NG)
            nc.vector.tensor_scalar(inv_g[:], deg[0:GC, 0:NG].rearrange("k (t q) -> k q t", q=QG), 1.0, None,
                                    ALU.max).then_inc(s_inv, 1)
            dve.wait_ge(s_inv, 1)
            nc.vector.reciprocal(inv_g[:], inv_g[:]).then_inc(s_inv, 1)

        @block.scalar
        def _(act):
            act.sem_inc(s_copied, 2)
            with act.Fori(0, T // 2) as t2:
                for q in range(PAIR):
                    half, part = q // QG, q % QG
                    act.wait_ge(s_group, PAIR * t2 + q + 1)
                    if part == 0:
                        act.wait_ge(s_c0, 2 * t2 + half + 1)
                        act.wait_ge(s_out[half], 16 * R * (t2 + 1))
                    for b in range(2):
                        n = min(SB, T - b * SB)
                        ins = nc.scalar.copy(
                            stage[half][:, :, b * SB:b * SB + n, part * GROUP:(part + 1) * GROUP]
                            .rearrange("p r t i -> p t r i"),
                            cnt_ps[q % 2][b][:, 0:n * GC].rearrange("p (t r i) -> p t r i", t=n, r=R))
                    ins.then_inc(s_copied, 1)

        @block.tensor
        def _(pe):
            pe.wait_ge(s_edge_f, 1)
            pe.wait_ge(s_const, N_CONST)
            for half in range(2):
                nc.tensor.transpose(misc[:, half * P:(half + 1) * P], edges[:, 0, half], ident[:])
                last = nc.tensor.transpose(misc[:, (2 + half) * P:(3 + half) * P], key[:, half], ident[:])
            last.then_inc(s_tr, 1)
            pe.wait_ge(s_spanb, 1)
            for m in range(2):
                nc.tensor.matmul(deg[0:NG, 256 * m:256 * m + P], span_b[:, 0, m, :], ident[:], start=True, stop=True)
                last = nc.tensor.matmul(deg[0:NG, 256 * m + P:256 * m + 2 * ETP], span_b[:, 1, m, :],
                                        ident[:, 0:2 * ETP - P],
                                        start=True, stop=True)
            last.then_inc(s_bc, 1)
            pe.wait_ge(s_row, 1)
            pe.wait_ge(s_cols, 1)
            nc.tensor.matmul(misc[0:1, 0:NG], rng[:, 2:3], ident[0:NG, 0:NG], start=True, stop=True)
            nc.tensor.matmul(misc[0:1, NG:2 * NG], rng[:, 3:4], tri[:], start=True, stop=False)
            nc.tensor.matmul(misc[0:1, NG:2 * NG], rng[:, 4:5], ident[0:NG, 0:NG], start=False,
                             stop=True).then_inc(s_pre, 1)
            pe.sem_inc(s_free, 2 * ETP + 2)
            pe.wait_ge(s_table, 2)
            nc.tensor.matmul(deg[0:GC, 0:NG], zero_b[:, 0:GC], zero_b[:, 0:NG], start=True, stop=False,
                             skip_group_check=True)
            read = ranges(pe)
            with pe.Fori(0, NG // 2) as g2:
                for q in range(2):
                    g = 2 * g2 + q
                    bank = cnt_ps[q]
                    pe.wait_ge(s_copied, g + 1)
                    for b in range(2):
                        nc.tensor.matmul(bank[b][:, 0:min(SB, T - b * SB) * GC], zero_b[:, 0:P],
                                         zero_b[:, 0:min(SB, T - b * SB) * GC], start=True, stop=False,
                                         skip_group_check=True)
                    lo, end, shift = read(g)
                    with pe.Fori(lo, end) as j:
                        v = j + shift
                        for tile in range(2):
                            pe.wait_ge(s_hot, 2 * v + tile + 1)
                            for s in range(T):
                                b, c = s // SB, s % SB
                                nc.tensor.matmul(bank[b][:, c * GC:(c + 1) * GC],
                                                 hot_src[:, tile, s * P:(s + 1) * P], hot_key[:, tile],
                                                 start=False, stop=True, skip_group_check=True)
                            nc.tensor.matmul(deg[0:GC, ds(g, 1)], hot_key[:, tile], ones_b[:], start=False, stop=True,
                                             skip_group_check=True).then_inc(s_free, 1)
                    pe.matmul(misc[:, 0:2], zero_b[:, 0:P], zero_b[:, 0:2], start=True, stop=True,
                              skip_group_check=True).then_inc(s_group, 1)


def norm_and_project(nc, A, ctx, sb, pb, sem, ident, inv_g, inv, h1e, x2_dram, dims):
    T, D, DK, H1, C1, R, QG = (dims[k] for k in ("T", "D", "DK", "H1", "C1", "R", "QG"))
    HALF = D // 2
    HH = H1 // 2
    x, w1, wu, gb, bu, s_x, s_w, s_gb = (dims[k] for k in ("x", "w1", "wu", "gb", "bu", "s_x", "s_w", "s_gb"))
    eps = sb(ctx, "eps", [P, 1], F32)
    h = [sb(ctx, f"h{i}", [P, D], F32) for i in range(2)]
    xhat = [sb(ctx, f"xhat{i}", [P, D], F32) for i in range(2)]
    hT = [sb(ctx, f"hT{i}", [P, DK, P], F32) for i in range(2)]
    xT = [sb(ctx, f"xT{i}", [P, DK, P], F32) for i in range(2)]
    x2 = [sb(ctx, f"x2_{i}", [P, D], F32) for i in range(2)]
    st = sb(ctx, "bn", [P, 2, 2, 2, 6], F32)
    mv = sb(ctx, "mean_var", [P, 2, 2, 6], F32)
    turn = pb(ctx, "turn_ps", [P, 2, 1024])
    y = pb(ctx, "y_ps", [P, 2, 512])
    hp = pb(ctx, "h1_ps", [P, 2, 512])

    s_eps, s_seen = (sem(ctx, n) for n in ("eps_set", "statistics_seen"))
    s_part = sem(ctx, "x_plus_hwu")
    s_inv = sem(ctx, "inv_in")
    s_d, s_var, s_sd, s_aff, s_h, s_xhat = (sem(ctx, n) for n in (
        "dve_step", "var_ready", "sd_ready", "affine_ready", "h_ready", "xhat_ready"))
    s_turn, s_hT, s_xT, s_y, s_h1p, s_h1, s_x2, = (sem(ctx, n) for n in (
        "turned", "hT_ready", "xT_ready", "y_done", "h1_done", "h1_copied", "x2_ready"))
    s_st = [sem(ctx, f"x2_stored{i}") for i in range(2)]

    with nc.Block() as block:
        @block.sync
        def _(sp):
            for i in range(2):
                sp.sem_inc(s_st[i], 16)
            for q in range(QG):
                for r in range(R):
                    sp.dma_start(inv[q * GROUP:(q + 1) * GROUP, r, :],
                                 inv_g[r * GROUP:(r + 1) * GROUP, q, :]).then_inc(s_inv, 16)
            with sp.Fori(0, T // 2) as t2:
                for i in range(2):
                    sp.wait_ge(s_x2, 2 * t2 + i + 2)
                    sp.dma_start(x2_dram[ds((2 * t2 + i) * P, P), :], x2[i][:]).then_inc(s_st[i], 16)
            for i in range(2):
                sp.wait_ge(s_st[i], 16 * (T // 2 + 1))
            sp.wait_ge(s_inv, 16 * QG * R)

        @block.gpsimd
        def _(pool):
            pool.memset(eps[:], EPS).then_inc(s_eps, 1)
            pool.memset(h1e[:, :, :, C1:C1 + 1], 1.0).then_inc(s_eps, 1)

        def steps(t2, i):
            return 2 * t2 + i

        @block.vector
        def _(dve):
            dve.wait_ge(s_x, 32)
            dve.wait_ge(s_w, 32)
            def norm(t, i, w, src):
                base = 4 * t + 2 * w
                m = mv[:, i, w, :]
                for c in range(2):
                    last = nc.vector.bn_stats(st[:, i, w, c, :], src[:, c * HALF:(c + 1) * HALF])
                last.then_inc(s_d, 1)
                dve.wait_ge(s_d, base + 1)
                dve.sem_inc(s_seen, 1)
                nc.vector.bn_aggr(m[:, 0:2], st[:, i, w].rearrange("p c s -> p (c s)")).then_inc(s_var, 1)
                dve.wait_ge(s_sd, 2 * t + w + 1)
                nc.vector.reciprocal(m[:, 3:4], m[:, 2:3]).then_inc(s_d, 1)
                dve.wait_ge(s_d, base + 2)
                nc.vector.scalar_tensor_tensor(m[:, 4:5], m[:, 0:1], -1.0, m[:, 3:4], ALU.mult,
                                               ALU.mult).then_inc(s_aff, 1)

            def front(t, i):
                norm(t, i, 0, x[:, ds(t, 1), :].rearrange("p o d -> p (o d)"))
                dve.wait_ge(s_h, t + 1)
                norm(t, i, 1, h[i])
                nc.vector.tensor_scalar(xhat[i][:], h[i][:], mv[:, i, 1, 0:1], mv[:, i, 1, 3:4],
                                        ALU.subtract, ALU.mult).then_inc(s_xhat, 1)

            def back(t, i, t2):
                xt = x[:, ds(t, 1), :].rearrange("p o d -> p (o d)")
                dve.wait_ge(s_y, t + 1)
                dve.wait_ge(s_st[i], 16 * (t2 + 1))
                nc.vector.tensor_tensor(x2[i][:].rearrange("p (c n) -> p c n", c=2), y[:, :, 0:HALF],
                                        xt.rearrange("p (c n) -> p c n", c=2), ALU.add).then_inc(s_part, 1)
                dve.wait_ge(s_part, t + 1)
                nc.vector.tensor_tensor(x2[i][:], x2[i][:], bu[:], ALU.add).then_inc(s_x2, 1)

            front(0, 0)
            with dve.Fori(0, T // 2 - 1) as t2:
                for i in range(2):
                    front(2 * t2 + i + 1, 1 - i)
                    back(2 * t2 + i, i, t2)
            front(T - 1, 1)
            for i in range(2):
                back(T - 2 + i, i, T // 2 - 1)

        @block.scalar
        def _(act):
            act.wait_ge(s_eps, 1)
            act.wait_ge(s_gb, 48)
            def front(t, i):
                xt = x[:, ds(t, 1), :].rearrange("p o d -> p (o d)")
                act.wait_ge(s_var, 2 * t + 1)
                nc.scalar.activation(mv[:, i, 0, 2:3], mv[:, i, 0, 1:2], ACT.Sqrt, bias=eps[:]).then_inc(s_sd, 1)
                act.wait_ge(s_aff, 2 * t + 1)
                nc.scalar.activation(h[i][:], xt, ACT.Relu, bias=mv[:, i, 0, 4:5],
                                     scale=mv[:, i, 0, 3:4]).then_inc(s_h, 1)
                act.wait_ge(s_var, 2 * t + 2)
                nc.scalar.activation(mv[:, i, 1, 2:3], mv[:, i, 1, 1:2], ACT.Sqrt, bias=eps[:]).then_inc(s_sd, 1)

            def back(t, i, following=None):
                act.wait_ge(s_turn, 2 * t + 1)
                nc.scalar.copy(hT[i][:].rearrange("p k n -> p (k n)"), turn[:, 0, 0:D]).then_inc(s_hT, 1)
                act.wait_ge(s_turn, 2 * t + 2)
                for k in range(DK):
                    last = nc.scalar.activation(xT[i][:, k, :], turn[:, 1, k * P:(k + 1) * P], ACT.Identity,
                                                bias=gb[:, 1, k:k + 1], scale=gb[:, 0, k:k + 1])
                last.then_inc(s_xT, 1)
                if following:
                    front(*following)
                act.wait_ge(s_h1p, t + 1)
                dst = h1e[:, ds(t, 1), :, 0:C1].rearrange("p o h c -> p (o h) c")
                for c in range(2):
                    last = nc.scalar.copy(dst[:, c * HH:(c + 1) * HH, :],
                                          hp[:, c, 0:HALF].rearrange("p (h c) -> p h c", h=HH))
                last.then_inc(s_h1, 1)

            front(0, 0)
            with act.Fori(0, T // 2 - 1) as t2:
                for i in range(2):
                    back(2 * t2 + i, i, (2 * t2 + i + 1, 1 - i))
            back(T - 2, 0, (T - 1, 1))
            back(T - 1, 1)

        @block.tensor
        def _(pe):
            pe.wait_ge(s_w, 32)
            pe.wait_ge(s_gb, 48)
            pe.sem_inc(s_h1, 1)
            pe.sem_inc(s_x2, 1)
            with pe.Fori(0, T // 2) as t2:
                for i in range(2):
                    t = 2 * t2 + i
                    pe.wait_ge(s_h, t + 1)
                    for k in range(DK):
                        last = nc.tensor.transpose(turn[:, 0, k * P:(k + 1) * P], h[i][:, k * P:(k + 1) * P], ident[:])
                    last.then_inc(s_turn, 1)
                    pe.wait_ge(s_xhat, t + 1)
                    for k in range(DK):
                        last = nc.tensor.transpose(turn[:, 1, k * P:(k + 1) * P], xhat[i][:, k * P:(k + 1) * P], ident[:])
                    last.then_inc(s_turn, 1)
                    pe.wait_ge(s_hT, t + 1)
                    pe.wait_ge(s_x2, t + 1)
                    for k in range(DK):
                        for c in range(2):
                            last = nc.tensor.matmul(y[:, c, 0:HALF], hT[i][:, k, :], wu[:, k, c * HALF:(c + 1) * HALF],
                                                    start=(k == 0), stop=(k == DK - 1))
                    last.then_inc(s_y, 1)
                    pe.wait_ge(s_xT, t + 1)
                    pe.wait_ge(s_h1, t + 1)
                    for k in range(DK):
                        for c in range(2):
                            last = nc.tensor.matmul(hp[:, c, 0:HALF], xT[i][:, k, :], w1[:, k, c * HALF:(c + 1) * HALF],
                                                    start=(k == 0), stop=(k == DK - 1))
                    last.then_inc(s_h1p, 1)


def gat_attention(nc, A, ctx, sb, pb, sem, ident, C0, neg, he, o, H, C, n, arow_dram, uvrow_dram, make_neg, dims):
    T, NP = dims["T"], dims["NP"]
    HT = H * T
    W = 5
    a_bc = sb(ctx, f"a_bc{n}", [P, 2, H, C], F32)
    b_bc = sb(ctx, f"b_bc{n}", [P, H, C], F32)
    sc = sb(ctx, f"scores{n}", [P, 2, H, T], F32)
    sc2 = sb(ctx, f"scores_leaky{n}", [P, H, T], F32)
    top = sb(ctx, f"top{n}", [P, H, T], F32)
    mx = sb(ctx, f"mx{n}", [P, H, T], F32)
    uv = sb(ctx, f"uv{n}", [P, H, 2, T], F32)
    arow = sb(ctx, f"arow{n}", [HT, P], F32)
    uvrow = sb(ctx, f"uvrow{n}", [2 * T, H, P], F32)
    big = sb(ctx, f"s_src_bc{n}", [P, W, NP], F32)
    uv_bc = [sb(ctx, f"uv_bc{n}{i}", [P, 2, NP], F32) for i in range(2)]
    rden = sb(ctx, f"rden{n}", [P, T], F32)
    junk = sb(ctx, f"junk{n}", [P, 2, NP], F32)
    acc = pb(ctx, f"acc{n}", [P, T, 256])
    tp = pb(ctx, f"turn{n}", [P, 1536])

    s_ab, s_junk, s_tr, s_row, s_rst, s_abc = (sem(ctx, f"{x}{n}") for x in (
        "ab_in", "reduced", "rows_turned", "rows_copied", "rows_stored", "s_src_bc_in"))
    s_ct, s_neg, s_d, s_uv = (sem(ctx, f"{x}{n}") for x in ("c0_turned", "neg_done", "dve_step", "uv_done"))
    s_uvin = [sem(ctx, f"uv_in{n}{i}") for i in range(2)]
    s_lin, s_z, s_e, s_w, s_used, s_o = (sem(ctx, f"{x}{n}") for x in (
        "linear_done", "z_done", "exp_done", "weight_done", "weight_used", "head_out"))
    assert H < W and 2 * HT <= P and T % W == 0

    with nc.Block() as block:
        @block.sync
        def _(sp):
            for i, name in enumerate(("src", "dst")):
                sp.dma_start(a_bc[:, i].rearrange("p h c -> p (h c)"),
                             A[f"L0_gnn_a_{name}{n}"].rearrange("(a h) c -> a (h c)", a=1)
                             .to_broadcast([P, H * C])).then_inc(s_ab, 16)
            sp.dma_start(b_bc[:].rearrange("p h c -> p (h c)"),
                         A[f"L0_gnn_b{n}"].rearrange("(a d) -> a d", a=1).to_broadcast([P, H * C])).then_inc(s_ab, 16)
            sp.wait_ge(s_row, 1)
            sp.dma_start(arow_dram, arow[:]).then_inc(s_rst, 16)
            sp.wait_ge(s_rst, 16)
            sp.dma_start(big[:, 0:H, :].rearrange("p h n -> p (h n)"),
                         arow_dram.rearrange("(a r) p -> a (r p)", a=1).to_broadcast([P, HT * P])).then_inc(s_abc, 16)
            rows = uvrow_dram.rearrange("(h r) p -> h (r p)", h=H)
            for h in range(H):
                sp.wait_ge(s_row, 2 + h)
                sp.dma_start(uvrow_dram[2 * T * h:2 * T * (h + 1)], uvrow[:, h]).then_inc(s_rst, 16)
                sp.wait_ge(s_rst, 16 * (h + 2))
                if h >= 2:
                    sp.wait_ge(s_z, T * (h - 1))
                sp.dma_start(uv_bc[h % 2][:].rearrange("p w n -> p (w n)"),
                             rows[h:h + 1].to_broadcast([P, 2 * NP])).then_inc(s_uvin[h % 2], 16)

        @block.vector
        def _(dve):
            dve.wait_ge(s_ab, 48)
            reductions = 0

            def reduce_product(size, in0, in1, start, op0, op1, to):
                nonlocal reductions
                if reductions >= 2:
                    dve.wait_ge(s_junk, reductions - 1)
                nc.vector.tensor_tensor_reduce(junk[:, reductions % 2, 0:size], in0, in1, 1.0, start, op0, op1,
                                               to).then_inc(s_junk, 1)
                reductions += 1

            for i in range(2):
                for h in range(H):
                    for t in range(T):
                        reduce_product(C, he[:, t, h, 0:C], a_bc[:, i, h, :], 0.0, ALU.mult, ALU.add,
                                       sc[:, i, h, t:t + 1])
            if make_neg:
                for t in range(T):
                    dve.wait_ge(s_ct, t + 1)
                    nc.vector.tensor_scalar(neg[:, t, :], tp[:, 0:NP], 0.0, NEG, ALU.is_equal,
                                            ALU.mult).then_inc(s_neg, 1)
                dve.wait_ge(s_neg, T)
            dve.wait_ge(s_junk, reductions)
            nc.vector.tensor_scalar(sc2[:], sc[:, 0], SLOPE, None, ALU.mult)
            dve.wait_ge(s_abc, 16)
            for h in range(H):
                for t in range(T):
                    reduce_product(NP, neg[:, t, :], big[:, h, :], -3e38, ALU.add, ALU.max, top[:, h, t:t + 1])
                dve.wait_ge(s_junk, reductions)
                nc.vector.tensor_tensor(top[:, h], top[:, h], sc[:, 1, h], ALU.add).then_inc(s_d, 1)
                dve.wait_ge(s_d, 2 * h + 1)
                nc.vector.scalar_tensor_tensor(mx[:, h], top[:, h], SLOPE, top[:, h], ALU.mult,
                                               ALU.max).then_inc(s_d, 1)
                dve.wait_ge(s_d, 2 * h + 2)
                nc.vector.tensor_tensor(uv[:, h, 0], sc[:, 1, h], mx[:, h], ALU.subtract)
                nc.vector.scalar_tensor_tensor(uv[:, h, 1], sc[:, 1, h], SLOPE, mx[:, h], ALU.mult,
                                               ALU.subtract).then_inc(s_uv, 1)

            def exponent(i):
                h, k = i // T, i % T
                if k == 0:
                    dve.wait_ge(s_uvin[h % 2], 16 * (h // 2 + 1))
                dve.wait_ge(s_lin, i + 1)
                nc.vector.scalar_tensor_tensor(big[:, i % W], uv_bc[h % 2][:, 0], sc[:, 0, h, k:k + 1],
                                               big[:, i % W], ALU.add, ALU.max).then_inc(s_z, 1)

            def take(h):
                dve.wait_ge(s_used, T * (h + 1))
                nc.vector.reciprocal(rden[:], acc[:, :, C:C + 1].rearrange("p t o -> p (t o)")).then_inc(s_d, 1)
                dve.wait_ge(s_d, 2 * H + 1 + h)
                for t in range(T):
                    nc.vector.scalar_tensor_tensor(o[:, t, h * C:(h + 1) * C], acc[:, t, 0:C], rden[:, t:t + 1],
                                                   b_bc[:, h], ALU.mult, ALU.add).then_inc(s_o, 1)

            exponent(0)
            for i in range(HT):
                if i + 1 < HT:
                    exponent(i + 1)
                dve.wait_ge(s_e, i + 1)
                nc.vector.scalar_tensor_tensor(big[:, i % W], big[:, i % W], 1.0, C0[:, i % T], ALU.min,
                                               ALU.mult).then_inc(s_w, 1)
                if i % T == 1 and i > T:
                    take(i // T - 1)
            take(H - 1)

        @block.scalar
        def _(act):
            act.wait_ge(s_tr, 1)
            nc.scalar.copy(arow[:], acc[0:HT, 0, 0:P]).then_inc(s_row, 1)
            for h in range(H):
                act.wait_ge(s_tr, 2 + h)
                nc.scalar.copy(uvrow[:, h], tp[0:2 * T, 512 * (h % 2):512 * (h % 2) + P]).then_inc(s_row, 1)
            act.wait_ge(s_uv, H)

            def linear(i):
                h, k = i // T, i % T
                if k == 0:
                    act.wait_ge(s_uvin[h % 2], 16 * (h // 2 + 1))
                if i >= W:
                    act.wait_ge(s_used, i - W + 1)
                nc.scalar.activation(big[:, i % W], uv_bc[h % 2][:, 1], ACT.Identity,
                                     bias=sc2[:, h, k:k + 1]).then_inc(s_lin, 1)

            linear(0)
            linear(1)
            for i in range(HT):
                if i + 2 < HT:
                    linear(i + 2)
                act.wait_ge(s_z, i + 1)
                nc.scalar.activation(big[:, i % W], big[:, i % W], ACT.Exp).then_inc(s_e, 1)

        @block.tensor
        def _(pe):
            pe.wait_ge(s_junk, HT)
            nc.tensor.transpose(acc[0:HT, 0, 0:P], sc[:, 0].rearrange("p h t -> p (h t)"), ident[:]).then_inc(s_tr, 1)
            if make_neg:
                for t in range(T):
                    if t:
                        pe.wait_ge(s_neg, t)
                    for s in range(T):
                        last = nc.tensor.transpose(tp[:, s * P:(s + 1) * P], C0[:, s, t * P:(t + 1) * P], ident[:])
                    last.then_inc(s_ct, 1)
            if make_neg:
                pe.wait_ge(s_neg, T)
            for h in range(H):
                pe.wait_ge(s_uv, h + 1)
                if h >= 2:
                    pe.wait_ge(s_row, h)
                nc.tensor.transpose(tp[0:2 * T, 512 * (h % 2):512 * (h % 2) + P],
                                    uv[:, h].rearrange("p w t -> p (w t)"), ident[:]).then_inc(s_tr, 1)
            pe.wait_ge(s_row, 1)
            for h in range(H):
                for k in range(T):
                    pe.wait_ge(s_w, h * T + k + 1)
                    for t in range(T):
                        if h and k == 0 and t % 2 == 0:
                            pe.wait_ge(s_o, T * (h - 1) + t + 2)
                        last = nc.tensor.matmul(acc[:, t, 0:C + 1], big[:, k % W, t * P:(t + 1) * P], he[:, k, h, :],
                                                start=(k == 0 and t % 2 == 0), stop=(k == T - 1),
                                                skip_group_check=True)
                    last.then_inc(s_used, 1)


def project2(nc, A, ctx, sb, pb, sem, ident, out1, h2e, dims):
    T, D, DK, H2, C2 = (dims[k] for k in ("T", "D", "DK", "H2", "C2"))
    w2 = sb(ctx, "w2", [P, DK, H2 * C2], F32)
    oT = [sb(ctx, f"oT{i}", [P, DK, P], F32) for i in range(2)]
    tp = [pb(ctx, f"o_turn{i}", [P, 1024]) for i in range(2)]
    hp = [pb(ctx, f"h2_ps{i}", [P, 512]) for i in range(2)]
    s_w, s_one, s_tr, s_oT, s_mm, s_h2 = (sem(ctx, x) for x in (
        "w2_in", "ones_set", "o_turned", "oT_copied", "h2_done", "h2_copied"))
    with nc.Block() as block:
        @block.sync
        def _(sp):
            sp.dma_start(w2[:], A["L0_gnn_W2"].rearrange("(k p) n -> p k n", p=P)).then_inc(s_w, 16)

        @block.gpsimd
        def _(pool):
            pool.memset(h2e[:, :, :, C2:C2 + 1], 1.0).then_inc(s_one, 1)

        @block.tensor
        def _(pe):
            pe.wait_ge(s_w, 16)

            def turn(t):
                if t >= 2:
                    pe.wait_ge(s_oT, t - 1)
                for k in range(DK):
                    last = nc.tensor.transpose(tp[t % 2][:, k * P:(k + 1) * P], out1[:, t, k * P:(k + 1) * P], ident[:])
                last.then_inc(s_tr, 1)

            turn(0)
            for t in range(T):
                if t + 1 < T:
                    turn(t + 1)
                pe.wait_ge(s_oT, t + 1)
                if t >= 2:
                    pe.wait_ge(s_h2, t - 1)
                for k in range(DK):
                    last = nc.tensor.matmul(hp[t % 2][:, 0:H2 * C2], oT[t % 2][:, k, :], w2[:, k, :],
                                            start=(k == 0), stop=(k == DK - 1))
                last.then_inc(s_mm, 1)

        @block.scalar
        def _(act):
            for t in range(T):
                act.wait_ge(s_tr, t + 1)
                if t >= 2:
                    act.wait_ge(s_mm, t - 1)
                nc.scalar.copy(oT[t % 2][:].rearrange("p k n -> p (k n)"), tp[t % 2][:, 0:D]).then_inc(s_oT, 1)

        @block.vector
        def _(dve):
            for t in range(T):
                dve.wait_ge(s_mm, t + 1)
                nc.vector.tensor_copy(h2e[:, t, :, 0:C2],
                                      hp[t % 2][:, 0:H2 * C2].rearrange("p (h c) -> p h c", h=H2)).then_inc(s_h2, 1)


def update_x(nc, A, ctx, sb, pb, sem, ident, out2, x2_dram, dims):
    T, D, HC = dims["T"], dims["D"], dims["H2"] * dims["C2"]
    HALF = D // 2
    K1 = HC - P
    wa = sb(ctx, "wu_a", [P, D], F32)
    wb = sb(ctx, "wu_b", [K1, D], F32)
    oa = [sb(ctx, f"out2T_a{i}", [P, P], F32) for i in range(2)]
    ob = [sb(ctx, f"out2T_b{i}", [K1, P], F32) for i in range(2)]
    part = [sb(ctx, f"x2_part{i}", [P, D], F32) for i in range(2)]
    tp = [pb(ctx, f"out2_turn{i}", [P, 256]) for i in range(2)]
    y = [pb(ctx, f"x2_ps{i}", [P, 1024]) for i in range(2)]
    s_w, s_tr, s_oT, s_mm, s_x2 = (sem(ctx, x) for x in ("wu2_in", "out2_turned", "out2T_copied", "y2_done", "x2_summed"))
    s_in = [sem(ctx, f"x2_part_in{i}") for i in range(2)]
    s_st = [sem(ctx, f"x2_final_stored{i}") for i in range(2)]
    with nc.Block() as block:
        @block.sync
        def _(sp):
            sp.dma_start(wa[:], A["L0_gnn_Wu"][D:D + P]).then_inc(s_w, 16)
            sp.dma_start(wb[:], A["L0_gnn_Wu"][D + P:D + HC]).then_inc(s_w, 16)

            def load(t):
                if t >= 2:
                    sp.wait_ge(s_st[t % 2], 16 * (t // 2))
                sp.dma_start(part[t % 2][:], x2_dram[t * P:(t + 1) * P]).then_inc(s_in[t % 2], 16)

            load(0)
            load(1)
            for t in range(T):
                sp.wait_ge(s_x2, t + 1)
                sp.dma_start(x2_dram[t * P:(t + 1) * P], part[t % 2][:]).then_inc(s_st[t % 2], 16)
                if t + 2 < T:
                    load(t + 2)
            for i in range(2):
                sp.wait_ge(s_st[i], 16 * (T // 2))

        @block.tensor
        def _(pe):
            pe.wait_ge(s_w, 32)

            def turn(t):
                if t >= 2:
                    pe.wait_ge(s_oT, t - 1)
                nc.tensor.transpose(tp[t % 2][:, 0:P], out2[:, t, 0:P], ident[:])
                nc.tensor.transpose(tp[t % 2][0:K1, P:2 * P], out2[:, t, P:HC], ident[:]).then_inc(s_tr, 1)

            turn(0)
            for t in range(T):
                if t + 1 < T:
                    turn(t + 1)
                pe.wait_ge(s_oT, t + 1)
                if t >= 2:
                    pe.wait_ge(s_x2, t - 1)
                for c in range(2):
                    dst = y[t % 2][:, 512 * c:512 * c + HALF]
                    nc.tensor.matmul(dst, oa[t % 2][:], wa[:, c * HALF:(c + 1) * HALF], start=True, stop=False)
                    last = nc.tensor.matmul(dst, ob[t % 2][:], wb[:, c * HALF:(c + 1) * HALF], start=False, stop=True)
                last.then_inc(s_mm, 1)

        @block.scalar
        def _(act):
            for t in range(T):
                act.wait_ge(s_tr, t + 1)
                if t >= 2:
                    act.wait_ge(s_mm, t - 1)
                nc.scalar.copy(oa[t % 2][:], tp[t % 2][:, 0:P])
                nc.scalar.copy(ob[t % 2][:], tp[t % 2][0:K1, P:2 * P]).then_inc(s_oT, 1)

        @block.vector
        def _(dve):
            for t in range(T):
                dve.wait_ge(s_mm, t + 1)
                dve.wait_ge(s_in[t % 2], 16 * (t // 2 + 1))
                p = part[t % 2][:].rearrange("p (c n) -> p c n", c=2)
                nc.vector.tensor_tensor(p, p, y[t % 2][:].rearrange("p (c n) -> p c n", c=2)[:, :, 0:HALF],
                                        ALU.add).then_inc(s_x2, 1)


def rgcn(nc, A, ctx, sb, pb, sem, ident, inv, x2_dram, counts_dram, out, dims):
    T, NP, N, D, DK, LAST, R = (dims[k] for k in ("T", "NP", "N", "D", "DK", "LAST", "R"))
    TD, D1 = dims["TD"], dims["D1"]
    KT = [D1 // P, D1 // P, DK]
    NO = [D1, D, D]
    NC = [n // 2 for n in NO]
    L = len(KT)
    KM, NM = max(KT), max(NC)
    TASKS, AGGS = 2 * (R + 1), 2 * R
    LAG = 2
    CS, BANKS = 5, 4
    piece0 = [TASKS * sum(KT[:i]) for i in range(L)]
    assert D1 == D + TD and TD == P and (2 * T) % BANKS == 0 and T % CS == 0

    hTh = sb(ctx, "hT_hi", [P, KM, NP], F32R)
    hTl = sb(ctx, "hT_lo", [P, KM, NP], F32R)
    acc = sb(ctx, "acc", [P, T, max(NO)], F32)
    xwh = sb(ctx, "xw_hi", [P, T, NM], F32R)
    xwl = sb(ctx, "xw_lo", [P, T, NM], F32R)
    wh = sb(ctx, "w_hi", [P, KM, NM], F32R)
    wl = sb(ctx, "w_lo", [P, KM, NM], F32R)
    raw = sb(ctx, "w_raw", [P, 2, NM], F32)
    cnt = sb(ctx, "count_slots", [P, CS, T * P], F32R)
    bias = sb(ctx, "bias_bc", [P, max(NO)], F32)
    emb = sb(ctx, "emb", [R, TD], F32)
    eps = sb(ctx, "eps3", [P, 1], F32)
    part_id = sb(ctx, "part_id", [R, 1], F32)
    st = sb(ctx, "bn3", [P, T, 2, 6], F32)
    mv = sb(ctx, "mean_var3", [P, 5, T], F32)
    tps = pb(ctx, "xw_ps", [P, BANKS, 512])
    aps = pb(ctx, "agg_ps", [P, 2, 1024])

    def agg_bank(i):
        return aps[:, (i % BANKS) // 2, 512 * (i % 2):512 * (i % 2) + 512]

    names = ("eps3_set", "emb_in", "mean_step", "affine3", "sd3", "h3_ready", "onehot_ready", "turned3", "hT_ready",
             "hT_hi_ready", "w_hi_ready", "w_lo_ready", "xw_done", "xw_free", "xw_hi_ready", "agg_done", "agg_free", "bias_set", "final")
    (s_set, s_emb, s_bn, s_aff, s_sd, s_h, s_hot, s_turn, s_hT, s_hTh, s_wh, s_wl, s_tps, s_tfree, s_xwh,
     s_aps, s_afree, s_bi, s_fin) = (sem(ctx, x) for x in names)
    s_x2 = [sem(ctx, f"x2_in{t}") for t in range(2)]
    s_raw = [sem(ctx, f"w_raw_in{i}") for i in range(2)]
    s_cnt = [sem(ctx, f"counts_in{i}") for i in range(CS)]
    s_bias, s_granted = sem(ctx, "bias_in"), sem(ctx, "count_slot_granted")
    s_res = [sem(ctx, f"x2_again{i}") for i in range(CS)]
    s_out = sem(ctx, "out_stored")
    walls = [A[f"w_all{i + 1}"] for i in range(L)]

    def piece(l, q, k):
        return piece0[l] + KT[l] * q + k

    def slot(l, parity, k):
        return (KT[l] * parity + k) % 2

    def raw_count(l, pair, parity, k):
        i = slot(l, parity, k)
        before = TASKS // 2 * sum(KT[:l])
        own = len([j for j in range(k + 1) if slot(l, parity, j) == i])
        if parity:
            own += len([j for j in range(KT[l]) if slot(l, 0, j) == i])
        return 16 * (before + own) + 16 * KT[l] * pair

    with nc.Block() as block:
        @block.sync
        def _(sp):
            for i, (a, b) in enumerate(((0, 2), (2, T))):
                sp.dma_start(acc[:, a:b, 0:D],
                             x2_dram[a * P:b * P].rearrange("(t p) d -> p t d", p=P)).then_inc(s_x2[i], 16)
            sp.dma_start(emb[:], A["L1_gnn_node_emb"]).then_inc(s_emb, 16)
            sp.wait_ge(s_set, 1)
            kinds = A["node_type_3"]
            full = (T - 1) * P
            types = acc[0:R, :, D:D + P].bitcast(I32)
            sp.dma_start(types[:, 0:T - 1, :], kinds[0:full].rearrange("(a t p) -> a t p", a=1, p=P)
                         .to_broadcast([R, T - 1, P])).then_inc(s_emb, 16)
            sp.dma_start(types[:, T - 1, 0:LAST], kinds[full:N].rearrange("(a p) -> a p", a=1)
                         .to_broadcast([R, LAST])).then_inc(s_emb, 16)

            def weights(l, q, matrix, c, parity):
                for k in range(KT[l]):
                    i = slot(l, parity, k)
                    p = piece(l, q, k)
                    if not (isinstance(p, int) and p < 2):
                        sp.wait_ge(s_wl, p - 1)
                    src = walls[l][matrix] if isinstance(matrix, int) else \
                        walls[l][ds(matrix, 1)].rearrange("o k n -> (o k) n")
                    sp.dma_start(raw[:, i, 0:NC[l]],
                                 src[k * P:(k + 1) * P, c * NC[l]:(c + 1) * NC[l]]).then_inc(s_raw[i], 16)

            for l in range(L):
                weights(l, 0, 0, 0, 0)
                with sp.Fori(0, R) as r:
                    weights(l, 2 * r + 1, r, 1, 1)
                    weights(l, 2 * r + 2, r + 1, 0, 0)
                weights(l, 2 * R + 1, R, 1, 1)
            sp.wait_ge(s_aps, L * AGGS * T + CS)
            for t in range(T + CS):
                if t >= CS:
                    sp.wait_ge(s_fin, t - CS + 1)
                    n = P if t - CS < T - 1 else LAST
                    sp.dma_start(out[(t - CS) * P:(t - CS) * P + n], acc[0:n, t - CS, 0:D]).then_inc(s_out, 16)
                if t < T:
                    sp.dma_start(cnt[:, t % CS, 0:D].bitcast(F32),
                                 x2_dram[t * P:(t + 1) * P]).then_inc(s_res[t % CS], 16)
            sp.wait_ge(s_out, 16 * T)

        @block.gpsimd
        def _(pool):
            pool.memset(acc[0:R, T - 1, D:D + P].bitcast(I32), 0).then_inc(s_set, 1)
            pool.memset(eps[:], EPS).then_inc(s_set, 1)
            pool.iota(part_id[:], [[1, 1]], base=0, channel_multiplier=1,
                      allow_small_or_imprecise_dtypes=True).then_inc(s_set, 1)
            for l in range(L):
                if l:
                    pool.wait_ge(s_bi, l)
                pool.dma_start(bias[:, 0:NO[l]], A[f"L1_gnn_b{l + 1}"].rearrange("(a d) -> a d", a=1)
                               .to_broadcast([P, NO[l]])).then_inc(s_bias, 16)
                with pool.Fori(0, R) as r:
                    for c in range(2):
                        for t in range(T):
                            g = AGGS * l + 2 * r + c
                            pool.wait_ge(s_aps, T * g + t + 1)
                            pool.sem_inc(s_granted, 1)
                            pool.dma_start(cnt[:, t % CS, :].bitcast(F32),
                                           counts_dram[ds(r, 1), t].rearrange("o p n -> (o p) n")
                                           ).then_inc(s_cnt[t % CS], 16)

        @block.tensor
        def _(pe):
            pe.sem_inc(s_aps, CS)
            pe.wait_ge(s_emb, 48)

            def turn(l, t):
                kt = KT[l]
                if l == 0:
                    pe.wait_ge(s_h, t + 1)
                    pe.wait_ge(s_hot, 1)
                else:
                    pe.wait_ge(s_tfree, T * (TASKS * l - 1) + t + 1 + BANKS)
                    if t < 2:
                        pe.wait_ge(s_afree, AGGS * T * l + BANKS)
                if t >= 2:
                    pe.wait_ge(s_hT, T * l + t - 1)
                for k in range(DK if l == 0 else kt):
                    last = nc.tensor.transpose(aps[:, t % 2, k * P:(k + 1) * P], acc[:, t, k * P:(k + 1) * P], ident[:])
                if l == 0:
                    last = nc.tensor.matmul(aps[:, t % 2, D:D + TD], emb[:], acc[0:R, t, D:D + P],
                                            start=True, stop=True, skip_group_check=True)
                last.then_inc(s_turn, 1)

            def transform_tile(l, q, parity, m, w):
                bank = tps[:, (T * parity + m) % BANKS, 0:NC[l]]
                pe.wait_ge(s_tfree, T * (TASKS * l + q) + m + 1)
                pe.wait_ge(s_hT, T * l + m + 1)
                for k in range(KT[l]):
                    if m == 0:
                        pe.wait_ge(s_wl, piece(l, q, k) + 1)
                    hi, lo = hTh[:, k, m * P:(m + 1) * P], hTl[:, k, m * P:(m + 1) * P]
                    nc.tensor.matmul(bank, hi, w[0][:, k, 0:NC[l]], start=(k == 0), stop=False)
                    nc.tensor.matmul(bank, hi, w[1][:, k, 0:NC[l]], start=False, stop=False)
                    last = nc.tensor.matmul(bank, lo, w[0][:, k, 0:NC[l]], start=False, stop=(k == KT[l] - 1))
                last.then_inc(s_tps, 1)

            def transform(l, q, parity):
                for m in range(T):
                    transform_tile(l, q, parity, m, (wh, wl))

            def aggregate(l, r, c):
                g = AGGS * l + 2 * r + c
                for t in range(T):
                    bank = agg_bank(T * c + t)[:, 0:NC[l]]
                    pe.wait_ge(s_afree, T * g + t + 1)
                    pe.wait_ge(s_cnt[t % CS], 16 * ((T // CS) * g + t // CS + 1))
                    for s in range(T):
                        if t == 0:
                            pe.wait_ge(s_tfree, T * (TASKS * l + 2 * r + c) + s + 1 + BANKS)
                        lhs = cnt[:, t % CS, s * P:(s + 1) * P]
                        nc.tensor.matmul(bank, lhs, xwh[:, s, 0:NC[l]], start=(s == 0), stop=False)
                        last = nc.tensor.matmul(bank, lhs, xwl[:, s, 0:NC[l]], start=False, stop=(s == T - 1))
                    last.then_inc(s_aps, 1)

            for t in range(T):
                turn(0, t)
            for l in range(L):
                with pe.Fori(0, R) as r:
                    for c in range(2):
                        transform(l, 2 * r + c, c)
                        aggregate(l, r, c)
                transform(l, 2 * R, 0)
                for m in range(T + LAG):
                    if m < T:
                        transform_tile(l, 2 * R + 1, 1, m, (xwh, xwl))
                    if m >= LAG and l + 1 < L:
                        turn(l + 1, m - LAG)

        @block.scalar
        def _(act):
            act.wait_ge(s_set, 3)
            act.wait_ge(s_bn, 2)
            nc.scalar.activation(mv[:, 2, :], mv[:, 1, :], ACT.Sqrt, bias=eps[:]).then_inc(s_sd, 1)
            act.wait_ge(s_aff, 1)
            for t in range(T):
                nc.scalar.activation(acc[:, t, 0:D], acc[:, t, 0:D], ACT.Relu, bias=mv[:, 4, t:t + 1],
                                     scale=mv[:, 3, t:t + 1]).then_inc(s_h, 1)

            def split_piece(l, pair, parity, k, w=wh):
                i = slot(l, parity, k)
                act.wait_ge(s_raw[i], raw_count(l, pair, parity, k))
                nc.scalar.copy(w[:, k, 0:NC[l]], raw[:, i, 0:NC[l]]).then_inc(s_wh, 1)

            def split(l, pair, parity):
                act.wait_ge(s_tps, T * (TASKS * l + 2 * pair + parity))
                for k in range(KT[l]):
                    split_piece(l, pair, parity, k)

            def turned(l, t):
                kt = KT[l]
                act.wait_ge(s_turn, T * l + t + 1)
                nc.scalar.activation(hTh[:, 0:kt, t * P:(t + 1) * P],
                                     aps[:, t % 2, 0:kt * P].rearrange("p (k n) -> p k n", k=kt),
                                     ACT.Copy if l == 0 else ACT.Relu).then_inc(s_hTh, 1)

            def hi_part(l, r, c):
                g = AGGS * l + 2 * r + c
                for m in range(T):
                    act.wait_ge(s_tps, T * (TASKS * l + 2 * r + c) + m + 1)
                    if m == 0:
                        act.wait_ge(s_aps, T * g + CS)
                    nc.scalar.copy(xwh[:, m, 0:NC[l]], tps[:, (T * c + m) % BANKS, 0:NC[l]]).then_inc(s_xwh, 1)

            for k in range(KT[0]):
                split_piece(0, 0, 0, k)
            for t in range(T):
                turned(0, t)
            for l in range(L):
                with act.Fori(0, R) as r:
                    hi_part(l, r, 0)
                    split(l, r, 1)
                    hi_part(l, r, 1)
                    split(l, r + 1, 0)
                act.wait_ge(s_aps, T * AGGS * (l + 1) + CS)
                for k in range(KT[l]):
                    split_piece(l, R, 1, k, xwh)
                if l + 1 < L:
                    act.wait_ge(s_tps, T * (TASKS * (l + 1) - 1))
                    for m in range(T):
                        if m < KT[l + 1]:
                            split_piece(l + 1, 0, 0, m)
                        turned(l + 1, m)

        @block.vector
        def _(dve):
            dve.sem_inc(s_tfree, BANKS)
            dve.sem_inc(s_afree, BANKS)
            for i, (a, b) in enumerate(((0, 2), (2, T))):
                dve.wait_ge(s_x2[i], 16)
                for t in range(a, b):
                    for c in range(2):
                        last = nc.vector.bn_stats(st[:, t, c, :], acc[:, t, c * (D // 2):(c + 1) * (D // 2)])
            last.then_inc(s_bn, 1)
            dve.wait_ge(s_bn, 1)
            for t in range(T):
                last = nc.vector.bn_aggr(mv[:, 0:2, t], st[:, t].rearrange("p c s -> p (c s)"))
            last.then_inc(s_bn, 1)
            dve.wait_ge(s_sd, 1)
            nc.vector.reciprocal(mv[:, 3, :], mv[:, 2, :]).then_inc(s_bn, 1)
            dve.wait_ge(s_bn, 3)
            nc.vector.scalar_tensor_tensor(mv[:, 4, :], mv[:, 0, :], -1.0, mv[:, 3, :], ALU.mult,
                                           ALU.mult).then_inc(s_aff, 1)
            dve.wait_ge(s_emb, 48)
            dve.wait_ge(s_set, 3)
            hot = acc[0:R, :, D:D + P]
            nc.vector.tensor_scalar(hot, hot.bitcast(I32), part_id[:], None, ALU.is_equal).then_inc(s_hot, 1)

            def split_piece(l, q, parity, k, w=(wh, wl)):
                dve.wait_ge(s_wh, piece(l, q, k) + 1)
                nc.vector.tensor_tensor(w[1][:, k, 0:NC[l]], raw[:, slot(l, parity, k), 0:NC[l]],
                                        w[0][:, k, 0:NC[l]].bitcast(F32), ALU.subtract).then_inc(s_wl, 1)

            def turned(l, t):
                kt = KT[l]
                dve.wait_ge(s_hTh, T * l + t + 1)
                hi = hTh[:, 0:kt, t * P:(t + 1) * P].bitcast(F32)
                lo = hTl[:, 0:kt, t * P:(t + 1) * P]
                ps = aps[:, t % 2, 0:kt * P].rearrange("p (k n) -> p k n", k=kt)
                if l == 0:
                    nc.vector.tensor_tensor(lo, ps, hi, ALU.subtract).then_inc(s_hT, 1)
                else:
                    nc.vector.scalar_tensor_tensor(lo, ps, 0.0, hi, ALU.max, ALU.subtract).then_inc(s_hT, 1)

            def start_acc(l):
                dve.wait_ge(s_bias, 16 * (l + 1))
                dve.wait_ge(s_turn, T * (l + 1))
                for t in range(T):
                    last = nc.vector.tensor_copy(acc[:, t, 0:NO[l]], bias[:, 0:NO[l]])
                last.then_inc(s_bi, 1)
                dve.wait_ge(s_bi, l + 1)

            def add_root(l, c, t):
                dve.wait_ge(s_tps, T * (TASKS * l + 2 * R + c) + t + 1)
                if c == 1 and t == 0:
                    dve.wait_ge(s_afree, T * AGGS * (l + 1) + BANKS)
                a = acc[:, t, c * NC[l]:(c + 1) * NC[l]]
                nc.vector.tensor_tensor(a, tps[:, (T * c + t) % BANKS, 0:NC[l]], a, ALU.add).then_inc(s_tfree, 1)

            def lo_part(l, r, c):
                for m in range(T):
                    g = AGGS * l + 2 * r + c
                    dve.wait_ge(s_xwh, T * g + m + 1)
                    nc.vector.tensor_tensor(xwl[:, m, 0:NC[l]], tps[:, (T * c + m) % BANKS, 0:NC[l]],
                                            xwh[:, m, 0:NC[l]].bitcast(F32), ALU.subtract).then_inc(s_tfree, 1)

            def add_means(l, r, c, nxt):
                for t in range(T):
                    if t < KT[l]:
                        split_piece(l, *nxt, t)
                    g = AGGS * l + 2 * r + c
                    dve.wait_ge(s_aps, T * g + t + 1 + CS)
                    a = acc[:, t, c * NC[l]:(c + 1) * NC[l]]
                    nc.vector.scalar_tensor_tensor(a, agg_bank(T * c + t)[:, 0:NC[l]], inv[:, ds(r, 1), t], a,
                                                   ALU.mult, ALU.add).then_inc(s_afree, 1)

            for k in range(KT[0]):
                split_piece(0, 0, 0, k)
            for t in range(T):
                turned(0, t)
            for l in range(L):
                start_acc(l)
                with dve.Fori(0, R) as r:
                    for c in range(2):
                        lo_part(l, r, c)
                        add_means(l, r, c, (2 * r + c + 1, 1 - c))
                for k in range(KT[l]):
                    split_piece(l, 2 * R + 1, 1, k, (xwh, xwl))
                for t in range(T):
                    add_root(l, 0, t)
                for m in range(T + LAG):
                    if m < T:
                        add_root(l, 1, m)
                    if l + 1 < L:
                        if m < KT[l + 1]:
                            split_piece(l + 1, 0, 0, m)
                        if m >= LAG:
                            turned(l + 1, m - LAG)
                    elif m >= LAG:
                        t = m - LAG
                        dve.wait_ge(s_tfree, T * (TASKS * L - 1) + t + 1 + BANKS)
                        dve.wait_ge(s_res[t % CS], 16 * (t // CS + 1))
                        nc.vector.scalar_tensor_tensor(acc[:, t, 0:D], acc[:, t, 0:D], 0.0,
                                                       cnt[:, t % CS, 0:D].bitcast(F32), ALU.max,
                                                       ALU.add).then_inc(s_fin, 1)


_OUT = ((1250, 768), "float32")


def kernel(**inputs):
    import numpy as np
    import concourse.bacc as bacc
    from concourse.bass_utils import run_bass_kernel_spmd

    nc = bacc.Bacc("TRN2", target_bir_lowering=False, num_devices=1)
    arrays, aps = {}, {}
    for i in (1, 2, 3):
        inputs[f"w_all{i}"] = np.concatenate([np.asarray(inputs.pop(f"L1_gnn_w_rel{i}")),
                                              np.asarray(inputs.pop(f"L1_gnn_w_root{i}"))[None]])
    for name, value in inputs.items():
        a = np.ascontiguousarray(value)
        arrays[f"in_{name}"] = a
        aps[name] = nc.dram_tensor(f"in_{name}", a.shape, mybir.dt.from_np(a.dtype), kind="ExternalInput").ap()
    out = nc.dram_tensor("out", _OUT[0], F32, kind="ExternalOutput").ap()
    gnn_kernel(nc, aps, out)
    r = run_bass_kernel_spmd(nc, [arrays], core_ids=[0])
    return r.results[0]["out"]
```
